# Optimizing a Trainium2 kernel written in Bass

```python
import numpy as np
import jax
import jax.numpy as jnp

def _softmax(x, axis=-1):
    return jax.nn.softmax(x, axis=axis)

def _gelu(x):
    return jax.nn.gelu(x, approximate=True)

def _silu(x):
    return jax.nn.silu(x)

def _sigmoid(x):
    return jax.nn.sigmoid(x)

def _layernorm(x, axis=-1, eps=1e-05):
    m = jnp.mean(x, axis=axis, keepdims=True)
    v = jnp.var(x, axis=axis, keepdims=True)
    return (x - m) / jnp.sqrt(v + eps)

def _scatter_add(tgt, idx, src, axis=0):
    return tgt.at[idx].add(src)

def _segment_sum(src, seg, n):
    return jax.ops.segment_sum(src, seg, n)
kernel_name = 'mk_adj_preln_d4_adj_r2_44f2d1'

def setup_inputs(seed: int=0):
    np.random.seed(seed)
    _w = jnp.asarray

    def _rec_inputs():
        import jax
        import jax.numpy as jnp
        _gk = jax.random.key(seed)
        x = -0.0003972 + 0.9999 * jax.random.normal(jax.random.fold_in(_gk, 1), (16, 512, 128), jnp.float32)
        _a = jax.random.bernoulli(jax.random.fold_in(_gk, 2), 0.03125, (16, 512, 512))
        adj = _a.astype(jnp.int32)
        return (x, adj)
    x, adj = _rec_inputs()

    def _L0_gnn_setup():
        import jax, jax.numpy as jnp
        import numpy as np
        LEAKY_ALPHA = 0.2
        NEG_INF = -9000000000000000.0
        key = jax.random.key(seed)
        ks = jax.random.split(key, 6)
        B, N, D = (256, 200, 128)
        h = jax.random.normal(ks[0], (B, N, D), dtype=jnp.float32)
        adj = jax.random.randint(ks[1], (B, N, N), 0, 5, dtype=jnp.int32)
        a_0 = jax.random.normal(ks[2], (D,), dtype=jnp.float32)
        a_1 = jax.random.normal(ks[3], (D,), dtype=jnp.float32)
        a_2 = jax.random.normal(ks[4], (D,), dtype=jnp.float32)
        a_3 = jax.random.normal(ks[5], (D,), dtype=jnp.float32)
        return {'h': h, 'adj': adj, 'a_0': a_0, 'a_1': a_1, 'a_2': a_2, 'a_3': a_3}
    _L0_gnn_all = _L0_gnn_setup()
    _L0_gnn_in = {k: v for k, v in _L0_gnn_all.items() if k in ('a_0', 'a_1', 'a_2', 'a_3')}
    del _L0_gnn_all

    def _L1_gnn_setup():
        import jax, jax.numpy as jnp
        import numpy as np
        B, N, F_IN, H, HID = (2, 512, 128, 4, 32)
        key = jax.random.key(seed)
        k1, k2, k3, k4 = jax.random.split(key, 4)
        node_feat = jax.random.normal(k1, (B, N, F_IN), dtype=jnp.float32)
        adj_mtx = jax.random.randint(k2, (B, N, N), 0, 2, dtype=jnp.int32)
        W = jax.random.normal(k3, (F_IN, H * HID), dtype=jnp.float32) * np.sqrt(2.0 / (F_IN + H * HID))
        Wa = jax.random.normal(k4, (H, HID), dtype=jnp.float32) * np.sqrt(2.0 / (H + HID))
        return {'node_feat': node_feat, 'adj_mtx': adj_mtx, 'W': W, 'Wa': Wa}
    _L1_gnn_all = _L1_gnn_setup()
    _L1_gnn_in = {k: v for k, v in _L1_gnn_all.items() if k in ('W', 'Wa')}
    del _L1_gnn_all

    def _L2_gnn_setup():
        import jax, jax.numpy as jnp
        import numpy as np
        B, D, FIN, FOUT, H = (16, 256, 128, 128, 8)
        NEG_INF = -9000000000000000.0
        key = jax.random.key(seed)
        k1, k2, k3, k4, k5 = jax.random.split(key, 5)
        x = jax.random.normal(k1, (B, D, FIN), dtype=jnp.float32)
        adj = jax.random.randint(k2, (B, D, D), 0, 2, dtype=jnp.int32)
        limW = float(np.sqrt(6.0 / (FIN + FOUT))) * 1.414
        W = jax.random.uniform(k3, (FIN, FOUT), minval=-limW, maxval=limW, dtype=jnp.float32)
        lima = float(np.sqrt(6.0 / (2 * FOUT + H))) * 1.414
        a_w = jax.random.uniform(k4, (H, 2 * FOUT), minval=-lima, maxval=lima, dtype=jnp.float32)
        a_b = jax.random.uniform(k5, (H,), minval=-0.05, maxval=0.05, dtype=jnp.float32)
        return {'input': x, 'adj': adj, 'W': W, 'a_w': a_w, 'a_b': a_b}
    _L2_gnn_all = _L2_gnn_setup()
    _L2_gnn_in = {k: v for k, v in _L2_gnn_all.items() if k in ('W', 'a_w', 'a_b')}
    del _L2_gnn_all

    def _L3_gnn_setup():
        import jax, jax.numpy as jnp
        import numpy as np
        NEG_INF = -9000000000000000.0
        key = jax.random.key(seed)
        k1, k2, k3, k4, k5 = jax.random.split(key, 5)
        B, N, F_in, F_out = (8, 1024, 128, 128)
        h = jax.random.normal(k1, (B, N, F_in), dtype=jnp.float32)
        adj = jax.random.randint(k2, (B, N, N), 0, 2, dtype=jnp.int32)
        W = jax.random.normal(k3, (F_out, F_in), dtype=jnp.float32) * (1.0 / np.sqrt(F_in))
        a1 = jax.random.normal(k4, (F_out,), dtype=jnp.float32) * (1.0 / np.sqrt(2 * F_out))
        a2 = jax.random.normal(k5, (F_out,), dtype=jnp.float32) * (1.0 / np.sqrt(2 * F_out))
        return {'h': h, 'adj': adj, 'W': W, 'a1': a1, 'a2': a2}
    _L3_gnn_all = _L3_gnn_setup()
    _L3_gnn_in = {k: v for k, v in _L3_gnn_all.items() if k in ('W', 'a1', 'a2')}
    del _L3_gnn_all
    return {'x': x, 'adj': adj, 'L0_gnn_a_0': _L0_gnn_in['a_0'], 'L0_gnn_a_1': _L0_gnn_in['a_1'], 'L0_gnn_a_2': _L0_gnn_in['a_2'], 'L0_gnn_a_3': _L0_gnn_in['a_3'], 'L1_gnn_W': _L1_gnn_in['W'], 'L1_gnn_Wa': _L1_gnn_in['Wa'], 'L2_gnn_W': _L2_gnn_in['W'], 'L2_gnn_a_w': _L2_gnn_in['a_w'], 'L2_gnn_a_b': _L2_gnn_in['a_b'], 'L3_gnn_W': _L3_gnn_in['W'], 'L3_gnn_a1': _L3_gnn_in['a1'], 'L3_gnn_a2': _L3_gnn_in['a2']}

def reference(x, adj, L0_gnn_a_0, L0_gnn_a_1, L0_gnn_a_2, L0_gnn_a_3, L1_gnn_W, L1_gnn_Wa, L2_gnn_W, L2_gnn_a_w, L2_gnn_a_b, L3_gnn_W, L3_gnn_a1, L3_gnn_a2):
    import jax
    import jax.numpy as jnp

    def _L0_gnn_ref(h, adj, a_0, a_1, a_2, a_3):
        import jax, jax.numpy as jnp
        import numpy as np
        LEAKY_ALPHA = 0.2
        NEG_INF = -9000000000000000.0

        def scores(a):
            return jax.nn.leaky_relu(jnp.einsum('bnd,bmd->bnm', h * a, h), negative_slope=LEAKY_ALPHA)
        alpha = jnp.full(adj.shape, jnp.float32(NEG_INF), dtype=h.dtype)
        for k, a in enumerate((a_0, a_1, a_2, a_3)):
            alpha = jnp.where(adj == k + 1, scores(a), alpha)
        alpha = jax.nn.softmax(alpha, axis=-1)
        return jnp.einsum('bnm,bmd->bnd', alpha, h)

    def _L1_gnn_ref(node_feat, adj_mtx, W, Wa):
        import jax, jax.numpy as jnp
        import numpy as np
        B, N, F_IN, H, HID = (2, 512, 128, 4, 32)
        b, n, _ = node_feat.shape
        h, hid = Wa.shape
        x = (node_feat @ W).reshape(b, n, h, hid).transpose(0, 2, 1, 3)
        s = jax.nn.leaky_relu(x[:, :, :, None, :] + x[:, :, None, :, :], negative_slope=0.2)
        e = jnp.einsum('bhijk,hk->bhij', s, Wa)
        e = jnp.where(adj_mtx[:, None, :, :] > 0, e, -jnp.inf)
        att = jax.nn.softmax(e, axis=-1)
        xp = jnp.einsum('bhij,bhjd->bhid', att, x)
        return xp.transpose(0, 2, 1, 3).reshape(b, n, h * hid)

    def _L2_gnn_ref(input, adj, W, a_w, a_b):
        import jax, jax.numpy as jnp
        import numpy as np
        B, D, FIN, FOUT, H = (16, 256, 128, 128, 8)
        NEG_INF = -9000000000000000.0
        h = input @ W
        F = h.shape[-1]
        a1, a2 = (a_w[:, :F], a_w[:, F:])
        s1 = jnp.einsum('bif,hf->bhi', h, a1)
        s2 = jnp.einsum('bjf,hf->bhj', h, a2)
        e = jax.nn.leaky_relu(s1[:, :, :, None] + s2[:, :, None, :] + a_b[None, :, None, None])
        att = jnp.where(adj[:, None, :, :] > 0, e, NEG_INF)
        att = jax.nn.softmax(att, axis=-1)
        h_prime = jnp.einsum('bhij,bjf->bif', att, h) / att.shape[1]
        return h_prime

    def _L3_gnn_ref(h, adj, W, a1, a2):
        import jax, jax.numpy as jnp
        import numpy as np
        NEG_INF = -9000000000000000.0
        Wh = jnp.einsum('bnf,of->bno', h, W)
        f = Wh @ a1
        g = Wh @ a2
        e = jax.nn.leaky_relu(f[:, :, None] + g[:, None, :], negative_slope=0.2)
        e = jnp.where(adj > 0, e, NEG_INF)
        attention = jax.nn.softmax(e, axis=2)
        h_prime = jnp.einsum('bij,bjo->bio', attention, Wh)
        return jax.nn.elu(h_prime)
    h = jnp.maximum(_layernorm(x, axis=-1), 0.0)
    x = x + _L0_gnn_ref(h, adj, L0_gnn_a_0, L0_gnn_a_1, L0_gnn_a_2, L0_gnn_a_3)
    h = jnp.maximum(_layernorm(x, axis=-1), 0.0)
    x = x + _L1_gnn_ref(h, adj, L1_gnn_W, L1_gnn_Wa)
    h = jnp.maximum(_layernorm(x, axis=-1), 0.0)
    x = x + _L2_gnn_ref(h, adj, L2_gnn_W, L2_gnn_a_w, L2_gnn_a_b)
    h = jnp.maximum(_layernorm(x, axis=-1), 0.0)
    x = x + _L3_gnn_ref(h, adj, L3_gnn_W, L3_gnn_a1, L3_gnn_a2)
    return x

_drawn_inputs = setup_inputs


def setup_inputs(seed=0):
    import zlib

    import numpy as np

    out = dict(_drawn_inputs(seed))
    spreads = {}
    factors = {'L2_gnn_a_b': 64.0, 'L3_gnn_a1': 8.0, 'L3_gnn_a2': 3.914}
    for name, (base, spread) in spreads.items():
        noise = np.random.default_rng([zlib.crc32(name.encode()), seed]).standard_normal(out[name].shape)
        drawn = base * np.exp(spread * noise) if base else spread * noise
        out[name] = jnp.asarray(drawn.astype(out[name].dtype))
    for name, factor in factors.items():
        out[name] = (out[name] * factor).astype(out[name].dtype)
    return out
```

```python
from contextlib import ExitStack

import numpy as np
import concourse.bass as bass
from concourse import mybir

ALU = mybir.AluOpType
ACT = mybir.ActivationFunctionType
AX = mybir.AxisListType
F32 = mybir.dt.float32
BF16 = mybir.dt.bfloat16
I32 = mybir.dt.int32
U8 = mybir.dt.uint8

P = 128
BATCH, NODES, DIM = 16, 512, 128
TILES = NODES // P
KINDS = 4
H1, HID = 4, 32
H2 = 8
GROUP = 32
GROUPS = NODES // GROUP
PER_TILE = P // GROUP
WIN = NODES // 2 + GROUP
MIRROR = GROUPS // 2 - 1
MW = MIRROR * GROUP
ROUNDS = GROUP // 4
SPLIT = 96
NEG = -9.0e15
SLOPE0, SLOPE1, SLOPE2, SLOPE3 = 0.2, 0.2, 0.01, 0.2
EPS = 1e-5
BIG = 3.0e38


def lift(slope):
    return (1.0 - slope) / slope


ACT_SHARE = 13
ON_ACT = [(r * ACT_SHARE) % GROUP < ACT_SHARE for r in range(GROUP)]


def build(nc, x, adj, a_k, w1, wa, w2, a_w, a_b, w3, a1, a2, out):
    with ExitStack() as ctx:
        def sb(name, shape, dt=F32):
            return ctx.enter_context(nc.sbuf_tensor(name, shape, dt))

        def sem(name):
            return ctx.enter_context(nc.semaphore(name))

        bank = [ctx.enter_context(nc.psum_tensor(f"bank{i}", [P, 512], F32)) for i in range(8)]

        ident = sb("ident", [P, P])
        ident_b = sb("ident_b", [P, P], BF16)
        spread = sb("spread", [P, PER_TILE, H1, GROUP], BF16)
        spread_f = sb("spread_f", [P, PER_TILE, P])
        gather = sb("gather", [P, PER_TILE, P])
        reorder = sb("reorder", [P, P])
        head_block = sb("head_block", [P, H1, HID])
        pick = sb("pick", [SPLIT, H2, P], BF16)
        pick1 = sb("pick1", [SPLIT, H1, GROUP], BF16)
        half = sb("half", [P, TILES])

        ak_row = sb("ak_row", [P, KINDS])
        w1_sb = sb("w1_sb", [DIM, H1 * HID])
        w1t = sb("w1t", [H1 * HID, DIM])
        wa_block = sb("wa_block", [P, H1])
        slot_w = sb("slot_w", [P, ROUNDS, H1, ROUNDS])
        v1 = sb("v1", [DIM, SPLIT])
        w2_sb = sb("w2_sb", [DIM, DIM])
        w2t = sb("w2t", [DIM, DIM])
        aw_sb = sb("aw_sb", [H2, 2 * DIM])
        awt = sb("awt", [DIM, 2, H2])
        v2i = sb("v2i", [DIM, H2])
        v2j = sb("v2j", [DIM, SPLIT])
        b2_row = sb("b2_row", [P, H2])
        w3_sb = sb("w3_sb", [DIM, DIM])
        w3t = sb("w3t", [DIM, DIM])
        a12 = sb("a12", [DIM, 2])
        v3i = sb("v3i", [DIM, 1])
        v3j = sb("v3j", [DIM, SPLIT])

        adj_i = sb("adj_i", [P, TILES, NODES], I32)
        mask_add = sb("mask_add", [P, TILES, 2 * NODES], BF16)
        mask_one = sb("mask_one", [P, TILES, NODES], BF16)
        is_kind = sb("is_kind", [P, KINDS - 1, TILES, NODES], U8)
        x_in = sb("x_in", [P, TILES, DIM])
        x_mid = [sb(f"x_mid{i}", [P, TILES, DIM]) for i in range(3)]
        x_out = sb("x_out", [P, TILES, DIM])
        stats = sb("stats", [P, TILES, 6])
        mean_var = sb("mean_var", [P, TILES, 2])
        var_eps = sb("var_eps", [P, TILES])
        rstd = sb("rstd", [P, TILES])
        x_norm = sb("x_norm", [P, TILES, DIM])
        h_row = sb("h_row", [P, TILES, DIM])
        h_t = sb("h_t", [P, NODES + P])
        h_ak = sb("h_ak", [P, KINDS, NODES])
        score0 = sb("score0", [P, TILES, NODES])
        nmax = sb("nmax", [P, 32])
        rsum = sb("rsum", [P, 32])
        rinv = sb("rinv", [P, 32])
        y_t = sb("y_t", [P, NODES + WIN])
        y_rot = sb("y_rot", [P, PER_TILE, 2 * TILES - 1, DIM])
        relu_s = sb("relu_s", [P, GROUP, WIN])
        d_raw = sb("d_raw", [P, 2, WIN])
        e1 = sb("e1", [P, GROUPS, NODES])
        mirror = sb("mirror", [P, GROUPS + MIRROR, MW])
        p1 = sb("p1", [P, 2, NODES])
        p_t = sb("p_t", [P, 2, TILES, P])
        o1 = sb("o1", [P, 2, H1, HID])
        parts = sb("parts", [SPLIT, 2 * NODES], BF16)
        part_r = sb("part_r", [SPLIT, NODES])
        part_m = sb("part_m", [SPLIT, NODES], BF16)
        ci = sb("ci", [P, TILES, H2])
        hw = sb("hw", [P, TILES, DIM])
        acc2 = sb("acc2", [P, 2, NODES])
        elu_y = sb("elu_y", [P, TILES, DIM])
        elu_n = sb("elu_n", [P, TILES, DIM])
        u2 = relu_s[:, :, :].rearrange("p a b -> p (a b)")[:, 0:2 * H2 * NODES].rearrange(
            "p (n j) -> p n j", j=NODES)

        w_in = sem("w_in"); aw_in = sem("aw_in")
        adj_in = sem("adj_in"); x_loaded = sem("x_loaded"); stored = sem("stored")
        const_made = sem("const_made"); const_step = sem("const_step")
        prep_pe = sem("prep_pe"); prep_dve = sem("prep_dve")
        masks_ready = sem("masks_ready"); mask_twice = sem("mask_twice")
        step = sem("step")
        stats_ready = sem("stats_ready"); rstd_ready = sem("rstd_ready")
        xn_ready = sem("xn_ready"); xnt_ready = sem("xnt_ready"); ht_ready = sem("ht_ready")
        x_free = sem("x_free")
        hak_ready = sem("hak_ready"); s0_ready = sem("s0_ready"); s0_copied = sem("s0_copied")
        s0_picked = sem("s0_picked")
        u_ready = sem("u_ready"); max_ready = sem("max_ready"); exp_ready = sem("exp_ready")
        z_ready = sem("z_ready")
        pt_ready = sem("pt_ready"); pt_copied = sem("pt_copied")
        attn_ready = sem("attn_ready"); attn_used = sem("attn_used")
        vec_ready = sem("vec_ready"); parts_ready = sem("parts_ready")
        proj_ready = sem("proj_ready"); proj_copied = sem("proj_copied")
        yt_ready = sem("yt_ready"); yt_copied = sem("yt_copied")
        relu_act = sem("relu_act"); relu_dve = sem("relu_dve"); rounds_done = sem("rounds_done")
        raw_copied = sem("raw_copied")
        ord_ready = sem("ord_ready"); ord_copied = sem("ord_copied")
        mirrored = sem("mirrored"); wrapped = sem("wrapped"); row_filled = sem("row_filled")
        m1_ready = sem("m1_ready"); z1_ready = sem("z1_ready"); p1_ready = sem("p1_ready")
        p1t_ready = sem("p1t_ready"); p1t_act = sem("p1t_act"); p1t_dve = sem("p1t_dve")
        o1_ready = sem("o1_ready"); o1_scaled = sem("o1_scaled"); x2_ready = sem("x2_ready")
        acc_ready = sem("acc_ready"); ci_ready = sem("ci_ready"); ci_copied = sem("ci_copied")
        dve_passed = sem("dve_passed"); pool_passed = sem("pool_passed"); pe_passed = sem("pe_passed")
        elu_in = sem("elu_in"); elu_exp = sem("elu_exp"); x4_ready = sem("x4_ready")

        block = ctx.enter_context(nc.Block())

        @block.sync
        def _(sp):
            def load(b):
                sp.wait_ge(masks_ready, b * 5 + 1)
                sp.dma_start(adj_i[:, :, :], adj[bass.ds(b, 1), :, :].rearrange(
                    "o (t p) j -> p (o t) j", p=P)).then_inc(adj_in, 16)
                sp.wait_ge(x_free, b + 1)
                sp.dma_start(x_in[:, :, :], x[bass.ds(b, 1), :, :].rearrange(
                    "o (t p) d -> p (o t) d", p=P)).then_inc(x_loaded, 16)

            def store(b):
                sp.wait_ge(x4_ready, b + 1)
                sp.dma_start(out[bass.ds(b, 1), :, :].rearrange("o (t p) d -> p (o t) d", p=P),
                             x_out[:, :, :]).then_inc(stored, 16)

            load(0)
            for k in range(KINDS):
                sp.dma_start(ak_row[:, k:k + 1], a_k[k].rearrange("(d o) -> d o", o=1)).then_inc(w_in, 16)
            sp.dma_start(w1_sb[:, :], w1).then_inc(w_in, 16)
            sp.dma_start(w2_sb[:, :], w2).then_inc(w_in, 16)
            sp.dma_start(w3_sb[:, :], w3).then_inc(w_in, 16)
            sp.dma_start(aw_sb[:, :], a_w).then_inc(w_in, 16)
            sp.dma_start(b2_row[:, :], a_b.rearrange("(o h) -> o h", o=1).broadcast_to([P, H2])).then_inc(w_in, 16)
            sp.dma_start(a12[:, 0:1], a1.rearrange("(d o) -> d o", o=1)).then_inc(w_in, 16)
            sp.dma_start(a12[:, 1:2], a2.rearrange("(d o) -> d o", o=1)).then_inc(w_in, 16)
            sp.wait_ge(const_made, 1)
            for h in range(H1):
                sp.dma_start(wa_block[HID * h:HID * (h + 1), h:h + 1],
                             wa[h:h + 1, :].rearrange("o d -> d o")).then_inc(w_in, 16)
            with sp.Fori(0, BATCH - 1) as b:
                load(b + 1)
                store(b)
            store(BATCH - 1)
            sp.wait_ge(stored, 16 * (BATCH + 1))

        W_LOADS = 16 * (KINDS + 7 + H1)

        @block.gpsimd
        def _(pool):
            g = nc.gpsimd
            g.memset(wa_block[:, :], 0.0).then_inc(const_made, 1)
            for n, t in enumerate((ident[:, :], ident_b[:, :], spread[:, :, :, :], reorder[:, :],
                                   pick[:, :, :], pick1[:, :, :], head_block[:, :, :])):
                g.memset(t, 0.0).then_inc(const_step, 1)
            g.memset(half[:, :], -0.5).then_inc(const_made, 1)
            pool.wait_ge(const_step, 7)

            def one_where_zero(t, base, pattern):
                return g.affine_select(out=t, in_=t, compare_op=ALU.not_equal, fill=1.0, base=base,
                                       pattern=pattern, channel_multiplier=1)
            one_where_zero(ident[:, :], 0, [[-1, P]]).then_inc(const_made, 1)
            one_where_zero(ident_b[:, :], 0, [[-1, P]]).then_inc(const_made, 1)
            one_where_zero(spread[:, :, :, :], 0, [[-GROUP, PER_TILE], [0, H1], [-1, GROUP]]).then_inc(const_made, 1)
            one_where_zero(reorder[:, :].rearrange("p (h c s) -> p h c s", h=H1, c=4), 0,
                           [[-ROUNDS, H1], [-GROUP, 4], [-1, ROUNDS]]).then_inc(const_made, 1)
            for part in range(3):
                if part:
                    pool.wait_ge(const_step, 7 + 2 * part)
                one_where_zero(pick[:, :, :], -32 * part, [[-1, H2], [0, P]]).then_inc(const_step, 1)
                one_where_zero(pick1[:, :, :], -32 * part, [[-1, H1], [0, GROUP]]).then_inc(const_step, 1)
            pool.wait_ge(const_step, 13)
            g.memset(rsum[:, :], 1.0).then_inc(const_made, 1)

            def rstd_of(n):
                pool.wait_ge(stats_ready, n)
                g.tensor_tensor(rstd[:, :], var_eps[:, :], half[:, :], ALU.pow).then_inc(rstd_ready, 1)

            with pool.Fori(0, BATCH) as b:
                rstd_of(b * 4 + 1)
                pool.wait_ge(masks_ready, b * 5 + 2)
                pool.sem_inc(pool_passed, 1)
                g.tensor_copy(mask_add[:, :, NODES:2 * NODES], mask_add[:, :, 0:NODES]).then_inc(mask_twice, 1)
                rstd_of(b * 4 + 2)
                pool.wait_ge(wrapped, b + 1)
                pool.sem_inc(pool_passed, 1)
                flat = mirror[:, :, :].rearrange("p q c -> p (q c)")
                for q in range(GROUPS):
                    at = q * MW + MW - GROUP
                    src = flat[:, at:at + MIRROR * (MW - GROUP)].rearrange(
                        "p (m c) -> p m c", c=MW - GROUP)[:, :, 0:GROUP]
                    g.tensor_copy(e1[:, q, WIN:NODES].rearrange("p (m c) -> p m c", c=GROUP),
                                  src).then_inc(row_filled, 1)
                rstd_of(b * 4 + 3)
                rstd_of(b * 4 + 4)

        CONST_MADE = 7

        @block.scalar
        def _(act):
            s = nc.scalar
            act.wait_ge(const_made, CONST_MADE)
            s.activation(elu_n[:, 0, :], ident[:, :], ACT.Exp).then_inc(elu_exp, 1)
            act.sem_inc(raw_copied, 2)
            act.sem_inc(ord_copied, 2)

            def transposed_h(n, b):
                act.wait_ge(xnt_ready, b * 4 + n + 1)
                ins = s.activation(h_t[:, 0:NODES], bank[7][:, :], ACT.Relu)
                if n == 1:
                    ins = s.activation(h_t[:, NODES:NODES + P], bank[7][:, 0:P], ACT.Relu)
                ins.then_inc(ht_ready, 1)

            def copy_pt(b, n):
                act.wait_ge(pt_ready, b * 12 + n + 1)
                s.copy(p_t[:, n % 2, :, :].rearrange("p t i -> p (t i)"), bank[4 + n % 2][:, :]).then_inc(pt_copied, 1)

            with act.Fori(0, BATCH) as b:
                transposed_h(0, b)
                for t in range(TILES + 3):
                    if t < TILES:
                        act.wait_ge(s0_ready, b * 16 + 4 * t + 1)
                        s.copy(score0[:, t, :], bank[0][:, :]).then_inc(s0_copied, 1)
                    if 1 <= t <= TILES:
                        act.wait_ge(s0_picked, b * 12 + 3 * t)
                        s.activation(u2[:, t - 1, :], score0[:, t - 1, :], ACT.Relu,
                                     scale=lift(SLOPE0)).then_inc(u_ready, 1)
                    if 2 <= t <= TILES + 1:
                        act.wait_ge(max_ready, b * 40 + t - 1)
                        s.activation(score0[:, t - 2, :], score0[:, t - 2, :], ACT.Exp, scale=-1.0,
                                     bias=nmax[:, t - 2:t - 1],
                                     accum_out=rsum[:, t - 2:t - 1]).then_inc(exp_ready, 1)
                    if t >= 3:
                        copy_pt(b, t - 3)

                transposed_h(1, b)
                act.wait_ge(yt_ready, b + 1)
                s.copy(y_t[:, 0:NODES], bank[2][:, :])
                s.copy(y_t[:, NODES:NODES + WIN], bank[2][:, 0:WIN]).then_inc(yt_copied, 1)
                for v in range(PER_TILE):
                    act.wait_ge(proj_ready, b * 6 + v + 1)
                    src = bank[(0, 1, 4, 5)[v]]
                    s.copy(y_rot[:, v, 0:TILES, :].rearrange("p t d -> p (t d)"), src[:, :])
                    s.copy(y_rot[:, v, TILES:2 * TILES - 1, :].rearrange("p t d -> p (t d)"),
                           src[:, 0:(TILES - 1) * DIM]).then_inc(proj_copied, 1)

                act.wait_ge(yt_copied, b + 1)
                with act.Fori(0, TILES) as G:
                    def copy_raw(v):
                        act.wait_ge(rounds_done, (b * 16 + G * 4 + v + 2) * ROUNDS)
                        s.copy(d_raw[:, v % 2, :], bank[v % 2][:, 0:WIN]).then_inc(raw_copied, 1)

                    def copy_ord(v):
                        act.wait_ge(ord_ready, b * 16 + G * 4 + v + 1)
                        s.copy(e1[:, bass.ds(G * 4 + v, 1), 0:WIN].rearrange("p o j -> p (o j)"),
                               bank[2 + v % 2][:, 0:WIN]).then_inc(ord_copied, 1)

                    for v in range(PER_TILE):
                        for r in range(GROUP):
                            if r == 10 and v:
                                copy_raw(v - 1)
                            if r == 20 and v:
                                copy_ord(v - 1)
                            if not ON_ACT[r]:
                                continue
                            i = (r % 4) * ROUNDS + r // 4
                            act.wait_ge(rounds_done, (b * 16 + G * 4 + v) * ROUNDS + r // 4 + 1)
                            s.activation(relu_s[:, i, :], y_t[:, bass.ds(G * P + v * GROUP, WIN)], ACT.Relu,
                                         bias=y_t[:, bass.ds(G * P + v * GROUP + i, 1)]).then_inc(relu_act, 1)
                    copy_raw(PER_TILE - 1)
                    copy_ord(PER_TILE - 1)

                for q in range(GROUPS + 1):
                    if q < GROUPS:
                        act.wait_ge(z1_ready, b * 16 + q + 1)
                        if q >= 2:
                            act.wait_ge(p1t_ready, b * 16 + q - 1)
                        s.activation(p1[:, q % 2, :], e1[:, q, :], ACT.Exp, scale=-1.0,
                                     bias=nmax[:, q:q + 1], accum_out=rsum[:, q:q + 1]).then_inc(p1_ready, 1)
                    if q >= 1 and (q - 1) % 2 == 0:
                        act.wait_ge(p1t_ready, b * 16 + q)
                        if q >= 3:
                            act.wait_ge(o1_ready, b * 16 + q - 2)
                        s.copy(p_t[:, (q - 1) % 2, :, :].rearrange("p t i -> p (t i)"),
                               bank[4 + (q - 1) % 2][:, :]).then_inc(p1t_act, 1)

                transposed_h(2, b)
                act.wait_ge(proj_ready, b * 6 + 5)
                s.copy(hw[:, :, :].rearrange("p t d -> p (t d)"), bank[5][:, :]).then_inc(proj_copied, 1)
                act.wait_ge(ci_copied, 2 * b + 1)
                for n in range(TILES * H2 + 2):
                    if n < TILES * H2:
                        t, h = n // H2, n % H2
                        act.wait_ge(z_ready, b * 36 + n + 1)
                        if t >= 2:
                            act.wait_ge(acc_ready, b * 32 + n - 2 * H2 + 1)
                        s.activation(u2[:, n % 16, :], bank[n % 4][:, :], ACT.Relu,
                                     bias=ci[:, t, h:h + 1], scale=lift(SLOPE2)).then_inc(u_ready, 1)
                    if n >= 2:
                        m = n - 2
                        act.wait_ge(max_ready, b * 40 + 4 + m + 1)
                        s.activation(u2[:, m % 16, :], u2[:, m % 16, :], ACT.Exp, scale=-1.0, bias=nmax[:, m:m + 1],
                                     accum_out=rsum[:, m:m + 1]).then_inc(exp_ready, 1)
                    if n % H2 == H2 - 1 and n >= 2 * H2:
                        copy_pt(b, 4 + n // H2 - 2)
                for t in range(TILES - 2, TILES):
                    copy_pt(b, 4 + t)

                transposed_h(3, b)
                act.wait_ge(proj_ready, b * 6 + 6)
                s.copy(hw[:, :, :].rearrange("p t d -> p (t d)"), bank[5][:, :]).then_inc(proj_copied, 1)
                act.wait_ge(ci_copied, 2 * b + 2)
                for t in range(TILES + 2):
                    if t < TILES:
                        act.wait_ge(z_ready, b * 36 + 32 + t + 1)
                        s.activation(u2[:, t, :], bank[t][:, :], ACT.Relu, bias=ci[:, t, 0:1],
                                     scale=lift(SLOPE3)).then_inc(u_ready, 1)
                    if 1 <= t <= TILES:
                        act.wait_ge(max_ready, b * 40 + 36 + t)
                        s.activation(score0[:, t - 1, :], score0[:, t - 1, :], ACT.Exp, scale=-1.0,
                                     bias=nmax[:, t - 1:t],
                                     accum_out=rsum[:, t - 1:t]).then_inc(exp_ready, 1)
                    if t >= 2:
                        copy_pt(b, 8 + t - 2)
                act.wait_ge(elu_in, b + 1)
                s.activation(elu_n[:, :, :], elu_n[:, :, :], ACT.Exp).then_inc(elu_exp, 1)

        @block.vector
        def _(dve):
            v_ = nc.vector
            dve.sem_inc(masks_ready, 1)
            dve.sem_inc(stored, 16)
            dve.sem_inc(x_free, 1)
            dve.wait_ge(const_made, CONST_MADE)
            dve.wait_ge(w_in, W_LOADS)
            v_.memset(slot_w[:, :, :, :], 0.0).then_inc(prep_dve, 1)
            v_.memset(v1[:, :], 0.0).then_inc(prep_dve, 1)
            v_.memset(v2j[:, :], 0.0).then_inc(prep_dve, 1)
            v_.memset(v3j[:, :], 0.0).then_inc(prep_dve, 1)
            v_.tensor_copy(spread_f[:, :, :], spread[:, :, :, :].rearrange("p v h i -> p v (h i)")).then_inc(prep_dve, 1)
            dve.wait_ge(prep_dve, 5)
            for h in range(H1):
                v_.memset(head_block[HID * h:HID * (h + 1), h, :], 1.0).then_inc(prep_dve, 1)
            for k in range(ROUNDS):
                v_.tensor_scalar(slot_w[:, k, :, k], wa_block[:, :], 1.0 - SLOPE1, None, ALU.mult).then_inc(prep_dve, 1)
            dve.wait_ge(prep_pe, 1)
            v_.tensor_copy(w1t[:, :], bank[0][:, 0:P]).then_inc(prep_dve, 1)
            v_.tensor_copy(w2t[:, :], bank[0][:, P:2 * P]).then_inc(prep_dve, 1)
            v_.tensor_copy(w3t[:, :], bank[0][:, 2 * P:3 * P]).then_inc(prep_dve, 1)
            v_.tensor_copy(awt[:, :, :].rearrange("p a h -> p (a h)"), bank[1][:, 0:2 * H2]).then_inc(prep_dve, 1)
            v_.tensor_copy(gather[:, :, :].rearrange("p v i -> p (v i)"), bank[2][:, :]).then_inc(prep_dve, 1)
            dve.wait_ge(prep_pe, 2)
            for part in range(3):
                c = 32 * part
                v_.tensor_scalar(v1[:, c:c + H1], bank[3][:, 0:H1], SLOPE1, None, ALU.mult).then_inc(prep_dve, 1)
                v_.tensor_copy(v2j[:, c:c + H2], bank[3][:, 16:16 + H2]).then_inc(prep_dve, 1)
                v_.tensor_copy(v3j[:, c:c + 1], bank[3][:, 33:34]).then_inc(prep_dve, 1)
            v_.tensor_scalar(v2i[:, :], bank[3][:, 8:8 + H2], lift(SLOPE2), None, ALU.mult).then_inc(prep_dve, 1)
            v_.tensor_scalar(v3i[:, :], bank[3][:, 32:33], lift(SLOPE3), None, ALU.mult).then_inc(prep_dve, 1)
            v_.tensor_scalar(b2_row[:, :], b2_row[:, :], lift(SLOPE2), None, ALU.mult).then_inc(prep_dve, 1)
            dve.wait_ge(prep_dve, 9 + ROUNDS + 5 + 12)

            STEPS = 30
            with dve.Fori(0, BATCH) as b:
                made = [0]

                def own(ins):
                    made[0] += 1
                    ins.then_inc(step, 1)
                    dve.wait_ge(step, b * STEPS + made[0])

                def leaky(to, lifted, u, slope, n):
                    dve.sem_inc(dve_passed, 1)
                    v_.tensor_tensor_reduce(to, lifted, u, -slope, BIG, ALU.add, ALU.min,
                                            nmax[:, n:n + 1]).then_inc(max_ready, 1)

                def layernorm(n, src):
                    for t in range(TILES):
                        ins = v_.bn_stats(stats[:, t, :], src[:, t, :])
                    own(ins)
                    dve.sem_inc(dve_passed, 1)
                    for t in range(TILES):
                        ins = v_.bn_aggr(mean_var[:, t, :], stats[:, t, :])
                    own(ins)
                    v_.tensor_scalar(var_eps[:, :], mean_var[:, :, 1], EPS, None, ALU.add).then_inc(stats_ready, 1)
                    dve.wait_ge(rstd_ready, b * 4 + n + 1)
                    for t in range(TILES):
                        ins = v_.tensor_scalar(x_norm[:, t, :], src[:, t, :], mean_var[:, t, 0:1],
                                               rstd[:, t:t + 1], ALU.subtract, ALU.mult)
                    ins.then_inc(xn_ready, 1)

                def split(n):
                    dve.wait_ge(vec_ready, b * 3 + n + 1)
                    own(v_.tensor_copy(parts[:, 0:NODES], bank[6][0:SPLIT, :]))
                    own(v_.tensor_tensor(part_r[:, :], bank[6][0:SPLIT, :], parts[:, 0:NODES], ALU.subtract))
                    own(v_.tensor_copy(part_m[:, :], part_r[:, :]))
                    own(v_.tensor_tensor(part_r[:, :], part_r[:, :], part_m[:, :], ALU.subtract))
                    v_.tensor_copy(parts[32:64, 0:NODES], part_m[32:64, :])
                    ins = v_.tensor_copy(parts[64:96, 0:NODES], part_r[64:96, :])
                    if n == 0:
                        own(ins)
                        ins = v_.tensor_copy(parts[:, NODES:2 * NODES], parts[:, 0:NODES])
                    ins.then_inc(parts_ready, 1)

                dve.wait_ge(adj_in, 16 * b + 16)
                v_.tensor_scalar(mask_add[:, :, 0:NODES], adj_i[:, :, :], 0, NEG, ALU.is_le,
                                 ALU.mult).then_inc(masks_ready, 1)
                v_.tensor_scalar(mask_one[:, :, :], adj_i[:, :, :], 1, NEG / SLOPE0, ALU.not_equal,
                                 ALU.mult).then_inc(masks_ready, 1)
                for k in range(1, KINDS):
                    v_.tensor_scalar(is_kind[:, k - 1, :, :], adj_i[:, :, :], k + 1, None,
                                     ALU.is_equal).then_inc(masks_ready, 1)

                dve.wait_ge(x_loaded, 16 * b + 16)
                layernorm(0, x_in)
                dve.wait_ge(xn_ready, b * 4 + 1)
                v_.tensor_scalar(h_row[:, :, :], x_norm[:, :, :], 0.0, None, ALU.max).then_inc(hak_ready, 1)
                dve.wait_ge(ht_ready, b * 4 + 1)
                for k in range(KINDS):
                    v_.tensor_scalar(h_ak[:, k, :], h_t[:, 0:NODES], ak_row[:, k:k + 1], None,
                                     ALU.mult).then_inc(hak_ready, 1)
                for t in range(TILES + 4):
                    if t < TILES:
                        for k in range(1, KINDS):
                            if k == 1:
                                dve.wait_ge(s0_copied, b * 4 + t + 1)
                            else:
                                dve.wait_ge(s0_picked, b * 12 + 3 * t + k - 1)
                            dve.wait_ge(s0_ready, b * 16 + 4 * t + k + 1)
                            dve.sem_inc(dve_passed, 1)
                            v_.copy_predicated(score0[:, t, :], is_kind[:, k - 1, t, :],
                                               bank[k][:, :]).then_inc(s0_picked, 1)
                    if 1 <= t <= TILES:
                        dve.wait_ge(u_ready, b * 40 + t)
                        leaky(score0[:, t - 1, :], u2[:, t - 1, :], score0[:, t - 1, :], SLOPE0, t - 1)
                    if t >= 4:
                        n = t - 4
                        if n == 0:
                            dve.wait_ge(exp_ready, b * 40 + 4)
                            own(v_.reciprocal(rinv[:, 0:TILES], rsum[:, 0:TILES]))
                        dve.wait_ge(attn_ready, b * 12 + n + 1)
                        v_.scalar_tensor_tensor(x_mid[0][:, n, :], bank[6 + n % 2][:, 0:P], rinv[:, n:n + 1],
                                                x_in[:, n, :], ALU.mult, ALU.add).then_inc(attn_used, 1)
                dve.wait_ge(attn_used, b * 12 + 4)
                layernorm(1, x_mid[0])
                split(0)
                dve.wait_ge(yt_copied, b + 1)
                dve.sem_inc(x_free, 1)
                with dve.Fori(0, TILES) as G:
                    for v in range(PER_TILE):
                        for r in range(GROUP):
                            if ON_ACT[r]:
                                continue
                            i = (r % 4) * ROUNDS + r // 4
                            dve.wait_ge(rounds_done, (b * 16 + G * 4 + v) * ROUNDS + r // 4 + 1)
                            v_.tensor_scalar(relu_s[:, i, :], y_t[:, bass.ds(G * P + v * GROUP, WIN)],
                                             y_t[:, bass.ds(G * P + v * GROUP + i, 1)], 0.0, ALU.add,
                                             ALU.max).then_inc(relu_dve, 1)
                for q in range(GROUPS):
                    dve.wait_ge(ord_copied, b * 16 + q + 3)
                    v_.transpose(mirror[:, q + MIRROR, :], e1[:, q, GROUP:GROUP + MW]).then_inc(mirrored, 1)
                dve.wait_ge(mirrored, b * 16 + 16)
                v_.tensor_copy(mirror[:, 0:MIRROR, :], mirror[:, GROUPS:GROUPS + MIRROR, :]).then_inc(wrapped, 1)
                for q in range(GROUPS + 3):
                    if q < GROUPS:
                        dve.wait_ge(row_filled, b * 16 + q + 1)
                        dve.wait_ge(m1_ready, b * 16 + q + 1)
                        dve.sem_inc(dve_passed, 1)
                        v_.tensor_tensor_reduce(e1[:, q, :], e1[:, q, :], bank[q % 2][:, :], -1.0, BIG, ALU.add,
                                                ALU.min, nmax[:, q:q + 1]).then_inc(z1_ready, 1)
                    if q >= 2 and q - 2 < GROUPS and (q - 2) % 2 == 1:
                        n = q - 2
                        dve.wait_ge(p1t_ready, b * 16 + n + 1)
                        dve.wait_ge(o1_ready, b * 16 + n - 1)
                        v_.tensor_copy(p_t[:, n % 2, :, :].rearrange("p t i -> p (t i)"),
                                       bank[4 + n % 2][:, :]).then_inc(p1t_dve, 1)
                    if q >= 3:
                        n = q - 3
                        dve.wait_ge(p1_ready, b * 16 + n + 1)
                        v_.reciprocal(rinv[:, n:n + 1], rsum[:, n:n + 1]).then_inc(o1_scaled, 1)
                        dve.wait_ge(o1_scaled, b * 32 + 2 * n + 1)
                        dve.wait_ge(o1_ready, b * 16 + n + 1)
                        if n >= 2:
                            dve.wait_ge(x2_ready, b * 16 + n - 1)
                        v_.scalar_tensor_tensor(o1[:, n % 2, :, :].rearrange("p h d -> p (h d)"),
                                                bank[(6, 2)[n % 2]][:, 0:P], rinv[:, n:n + 1],
                                                head_block[:, :, :].rearrange("p h d -> p (h d)"),
                                                ALU.mult, ALU.mult).then_inc(o1_scaled, 1)
                dve.wait_ge(x2_ready, b * 16 + 16)
                own(v_.tensor_tensor(x_mid[1][:, :, :].rearrange("p t d -> p (t d)"), bank[7][:, :],
                                     x_mid[0][:, :, :].rearrange("p t d -> p (t d)"), ALU.add))
                layernorm(2, x_mid[1])
                split(1)
                dve.wait_ge(ci_ready, 2 * b + 1)
                v_.tensor_tensor(ci[:, :, :], bank[7][:, 0:TILES * H2].rearrange("p (t h) -> p t h", h=H2),
                                 b2_row[:, None, :].broadcast_to([P, TILES, H2]), ALU.add).then_inc(ci_copied, 1)
                def add_attended(t):
                    dve.wait_ge(attn_ready, b * 12 + 4 + t + 1)
                    v_.scalar_tensor_tensor(x_mid[2][:, t, :], bank[6 + t % 2][:, 0:P], 1.0 / H2,
                                            x_mid[1][:, t, :], ALU.mult, ALU.add).then_inc(attn_used, 1)

                for t in range(TILES + 2):
                    for h in range(H2):
                        if t < TILES:
                            n = H2 * t + h
                            dve.wait_ge(u_ready, b * 40 + 4 + n + 1)
                            leaky(u2[:, n % 16, :], u2[:, n % 16, :], bank[n % 4][:, :], SLOPE2, n)
                        if 1 <= t <= TILES:
                            n = H2 * (t - 1) + h
                            if h == 0:
                                dve.wait_ge(exp_ready, b * 40 + 4 + H2 * t)
                                own(v_.reciprocal(rinv[:, H2 * (t - 1):H2 * t], rsum[:, H2 * (t - 1):H2 * t]))
                            at = acc2[:, (t - 1) % 2, :]
                            if h == 0:
                                if t >= 3:
                                    dve.wait_ge(pt_ready, b * 12 + 4 + t - 2)
                                v_.tensor_scalar(at, u2[:, n % 16, :], rinv[:, n:n + 1], None,
                                                 ALU.mult).then_inc(acc_ready, 1)
                            else:
                                dve.wait_ge(acc_ready, b * 32 + n)
                                v_.scalar_tensor_tensor(at, u2[:, n % 16, :], rinv[:, n:n + 1], at, ALU.mult,
                                                        ALU.add).then_inc(acc_ready, 1)
                    if t >= 3:
                        add_attended(t - 3)
                for t in range(TILES - 1, TILES):
                    add_attended(t)
                dve.wait_ge(attn_used, b * 12 + 8)
                layernorm(3, x_mid[2])
                split(2)
                dve.wait_ge(ci_ready, 2 * b + 2)
                v_.tensor_copy(ci[:, :, 0], bank[7][:, 0:TILES]).then_inc(ci_copied, 1)
                for t in range(TILES):
                    dve.wait_ge(u_ready, b * 40 + 36 + t + 1)
                    leaky(score0[:, t, :], u2[:, t, :], bank[t][:, :], SLOPE3, t)
                dve.wait_ge(exp_ready, b * 40 + 40)
                own(v_.reciprocal(rinv[:, 0:TILES], rsum[:, 0:TILES]))
                for t in range(TILES):
                    dve.wait_ge(attn_ready, b * 12 + 8 + t + 1)
                    v_.tensor_scalar(elu_y[:, t, :], bank[6 + t % 2][:, 0:P], rinv[:, t:t + 1], None,
                                     ALU.mult).then_inc(attn_used, 1)
                dve.wait_ge(attn_used, b * 12 + 12)
                v_.tensor_scalar(elu_n[:, :, :], elu_y[:, :, :], 0.0, None, ALU.min).then_inc(elu_in, 1)
                v_.tensor_scalar(elu_y[:, :, :], elu_y[:, :, :], 0.0, -1.0, ALU.max, ALU.add).then_inc(step, 1)
                made[0] += 1
                dve.wait_ge(elu_exp, b + 2)
                dve.wait_ge(step, b * STEPS + made[0])
                own(v_.tensor_tensor(elu_y[:, :, :], elu_y[:, :, :], elu_n[:, :, :], ALU.add))
                dve.wait_ge(stored, b * 16 + 16)
                v_.tensor_tensor(x_out[:, :, :], elu_y[:, :, :], x_mid[2][:, :, :], ALU.add).then_inc(x4_ready, 1)
                assert made[0] == STEPS

        @block.tensor
        def _(pe):
            T = nc.tensor
            pe.sem_inc(rounds_done, ROUNDS)
            pe.wait_ge(const_made, CONST_MADE)
            pe.wait_ge(w_in, W_LOADS)
            pe.wait_ge(prep_dve, 5)
            for n, w in enumerate((w1_sb, w2_sb, w3_sb)):
                T.transpose(bank[0][:, n * P:(n + 1) * P], w[:, :], ident[:, :])
            for n in range(2):
                T.transpose(bank[1][:, n * H2:(n + 1) * H2], aw_sb[:, n * DIM:(n + 1) * DIM], ident[0:H2, 0:H2])
            for v in range(PER_TILE):
                ins = T.transpose(bank[2][:, v * P:(v + 1) * P], spread_f[:, v, :], ident[:, :])
            ins.then_inc(prep_pe, 1)
            pe.wait_ge(prep_dve, 9 + ROUNDS + 5)

            def mm(o, l, r, start=True, stop=True):
                return T.matmul(o, l, r, start=start, stop=stop, skip_group_check=True)
            mm(bank[3][:, 0:H1], w1t[:, :], wa_block[:, :])
            mm(bank[3][:, 8:8 + H2], w2t[:, :], awt[:, 0, :])
            mm(bank[3][:, 16:16 + H2], w2t[:, :], awt[:, 1, :])
            mm(bank[3][:, 32:34], w3_sb[:, :], a12[:, :]).then_inc(prep_pe, 1)
            pe.wait_ge(prep_dve, 9 + ROUNDS + 5 + 11)

            with pe.Fori(0, BATCH) as b:
                def turn_x(n):
                    pe.wait_ge(xn_ready, b * 4 + n + 1)
                    for t in range(TILES):
                        ins = T.transpose(bank[7][:, t * P:(t + 1) * P], x_norm[:, t, :], ident[:, :])
                    ins.then_inc(xnt_ready, 1)

                def turn_p(n, src):
                    for t in range(TILES):
                        ins = T.transpose(bank[4 + n % 2][:, t * P:(t + 1) * P], src[:, t * P:(t + 1) * P],
                                          ident[:, :])
                    ins.then_inc(pt_ready, 1)

                def attend(n, values):
                    pe.wait_ge(pt_copied, b * 12 + n + 1)
                    if n % TILES >= 2:
                        pe.wait_ge(attn_used, b * 12 + n - 1)
                    for t in range(TILES):
                        ins = mm(bank[6 + n % 2][:, 0:P], p_t[:, n % 2, t, :], values[:, t, :],
                                 t == 0, t == TILES - 1)
                    ins.then_inc(attn_ready, 1)

                turn_x(0)
                for t in range(TILES + 3):
                    if t < TILES:
                        for k in range(KINDS):
                            pe.wait_ge(hak_ready, b * 5 + 1 + k + 1)
                            if t == 0 and k == 0:
                                pe.wait_ge(masks_ready, b * 5 + 3)
                            if t:
                                if k == 0:
                                    pe.wait_ge(s0_copied, b * 4 + t)
                                else:
                                    pe.wait_ge(s0_picked, b * 12 + 3 * (t - 1) + k)
                            ins = mm(bank[k][:, :], h_ak[:, k, t * P:(t + 1) * P], h_t[:, 0:NODES], True, k > 0)
                            if k == 0:
                                ins = mm(bank[0][:, :], ident_b[:, :], mask_one[:, t, :], False, True)
                            ins.then_inc(s0_ready, 1)
                    if 2 <= t <= TILES + 1:
                        n = t - 2
                        pe.wait_ge(exp_ready, b * 40 + n + 1)
                        if n >= 2:
                            pe.wait_ge(pt_copied, b * 12 + n - 1)
                        turn_p(n, score0[:, n, :])
                    if t >= 3:
                        attend(t - 3, h_row)

                turn_x(1)
                pe.wait_ge(ht_ready, b * 4 + 2)
                mm(bank[2][:, :], w1_sb[:, :], h_t[:, 0:NODES]).then_inc(yt_ready, 1)
                mm(bank[6][0:SPLIT, :], v1[:, :], h_t[:, 0:NODES]).then_inc(vec_ready, 1)
                for v in range(PER_TILE):
                    for t in range(TILES):
                        at = v * GROUP + t * P
                        ins = mm(bank[(0, 1, 4, 5)[v]][:, t * P:(t + 1) * P], h_t[:, at:at + P], w1_sb[:, :])
                    ins.then_inc(proj_ready, 1)
                pe.wait_ge(proj_copied, b * 6 + 4)
                pe.sem_inc(pe_passed, 1)
                with pe.Fori(0, TILES) as G:
                    def put_in_order(v):
                        pe.wait_ge(raw_copied, b * 16 + G * 4 + v + 3)
                        pe.wait_ge(ord_copied, b * 16 + G * 4 + v + 1)
                        mm(bank[2 + v % 2][:, 0:WIN], reorder[:, :], d_raw[:, v % 2, :]).then_inc(ord_ready, 1)

                    for v in range(PER_TILE):
                        pe.wait_ge(raw_copied, b * 16 + G * 4 + v + 1)
                        for rnd in range(ROUNDS):
                            if rnd == 4 and v:
                                put_in_order(v - 1)
                            on_act = sum(ON_ACT[0:4 * rnd + 4])
                            pe.wait_ge(relu_act, (b * 16 + G * 4 + v) * ACT_SHARE + on_act)
                            pe.wait_ge(relu_dve, (b * 16 + G * 4 + v) * (GROUP - ACT_SHARE) + 4 * rnd + 4 - on_act)
                            for c in range(4):
                                ins = mm(bank[v % 2][32 * c:32 * c + 32, 0:WIN],
                                         slot_w[:, rnd, :, :].rearrange("p h s -> p (h s)"),
                                         relu_s[:, c * ROUNDS + rnd, :], rnd == 0, rnd == ROUNDS - 1)
                            ins.then_inc(rounds_done, 1)
                    put_in_order(PER_TILE - 1)

                pe.wait_ge(mask_twice, b + 1)
                pe.wait_ge(parts_ready, b * 3 + 1)
                pe.wait_ge(raw_copied, b * 16 + 16 + 2)
                for q in range(GROUPS + 3):
                    if q < GROUPS:
                        if q >= 2:
                            pe.wait_ge(z1_ready, b * 16 + q - 1)
                        mm(bank[q % 2][:, :], spread[:, q % PER_TILE, :, :].rearrange("p h i -> p (h i)"),
                           mask_add[:, q // PER_TILE, q * GROUP:q * GROUP + NODES], True, False)
                        mm(bank[q % 2][:, :], pick1[:, :, :].rearrange("p h i -> p (h i)"),
                           parts[:, q * GROUP:q * GROUP + NODES], False, True).then_inc(m1_ready, 1)
                    if 1 <= q <= GROUPS:
                        n = q - 1
                        pe.wait_ge(p1_ready, b * 16 + n + 1)
                        if n >= 2:
                            pe.wait_ge((p1t_act, p1t_dve)[n % 2], b * 8 + n // 2)
                        for t in range(TILES):
                            ins = T.transpose(bank[4 + n % 2][:, t * P:(t + 1) * P],
                                              p1[:, n % 2, t * P:(t + 1) * P], ident[:, :])
                        ins.then_inc(p1t_ready, 1)
                    if 2 <= q <= GROUPS + 1:
                        n = q - 2
                        pe.wait_ge((p1t_act, p1t_dve)[n % 2], b * 8 + n // 2 + 1)
                        if n >= 2:
                            pe.wait_ge(o1_scaled, b * 32 + 2 * (n - 2) + 2)
                        for t in range(TILES):
                            ins = mm(bank[(6, 2)[n % 2]][:, 0:P], p_t[:, n % 2, t, :],
                                     y_rot[:, n % PER_TILE, n // PER_TILE + t, :], t == 0, t == TILES - 1)
                        ins.then_inc(o1_ready, 1)
                    if q >= 3:
                        n = q - 3
                        pe.wait_ge(o1_scaled, b * 32 + 2 * n + 2)
                        tile = n // PER_TILE
                        ins = mm(bank[7][:, tile * P:(tile + 1) * P], gather[:, n % PER_TILE, :],
                                 o1[:, n % 2, :, :].rearrange("p h d -> p (h d)"), n % PER_TILE == 0,
                                 n % PER_TILE == PER_TILE - 1)
                        ins.then_inc(x2_ready, 1)

                turn_x(2)
                pe.wait_ge(ht_ready, b * 4 + 3)
                mm(bank[6][0:SPLIT, :], v2j[:, :], h_t[:, 0:NODES]).then_inc(vec_ready, 1)
                for t in range(TILES):
                    ins = mm(bank[7][:, t * H2:(t + 1) * H2], h_t[:, t * P:(t + 1) * P], v2i[:, :])
                ins.then_inc(ci_ready, 1)
                for t in range(TILES):
                    ins = mm(bank[5][:, t * P:(t + 1) * P], h_t[:, t * P:(t + 1) * P], w2_sb[:, :])
                ins.then_inc(proj_ready, 1)
                pe.wait_ge(parts_ready, b * 3 + 2)
                for t in range(TILES + 2):
                    for h in range(H2):
                        n = H2 * t + h
                        if t < TILES:
                            if n >= 4:
                                pe.wait_ge(max_ready, b * 40 + 4 + n - 3)
                            mm(bank[n % 4][:, :], pick[:, h, :], parts[:, 0:NODES], True, False)
                            mm(bank[n % 4][:, :], ident_b[:, :], mask_add[:, t, 0:NODES], False,
                               True).then_inc(z_ready, 1)
                        if h == 3 and t >= 2:
                            m = t - 2
                            pe.wait_ge(acc_ready, b * 32 + H2 * (m + 1))
                            if m == 0:
                                pe.wait_ge(proj_copied, b * 6 + 5)
                            if m >= 2:
                                pe.wait_ge(pt_copied, b * 12 + 4 + m - 1)
                            turn_p(4 + m, acc2[:, m % 2, :])
                        if h == 7 and t >= 2:
                            attend(4 + t - 2, hw)

                turn_x(3)
                pe.wait_ge(ht_ready, b * 4 + 4)
                mm(bank[6][0:SPLIT, :], v3j[:, :], h_t[:, 0:NODES]).then_inc(vec_ready, 1)
                for t in range(TILES):
                    ins = mm(bank[7][:, t:t + 1], h_t[:, t * P:(t + 1) * P], v3i[:, :])
                ins.then_inc(ci_ready, 1)
                for t in range(TILES):
                    ins = mm(bank[5][:, t * P:(t + 1) * P], h_t[:, t * P:(t + 1) * P], w3t[:, :])
                ins.then_inc(proj_ready, 1)
                pe.wait_ge(parts_ready, b * 3 + 3)
                for t in range(TILES):
                    mm(bank[t][:, :], pick[:, 0, :], parts[:, 0:NODES], True, False)
                    mm(bank[t][:, :], ident_b[:, :], mask_add[:, t, 0:NODES], False, True).then_inc(z_ready, 1)
                pe.wait_ge(proj_copied, b * 6 + 6)
                for t in range(TILES):
                    pe.wait_ge(exp_ready, b * 40 + 36 + t + 1)
                    if t >= 2:
                        pe.wait_ge(pt_copied, b * 12 + 8 + t - 1)
                    turn_p(8 + t, score0[:, t, :])
                    if t:
                        attend(8 + t - 1, hw)
                attend(11, hw)


INPUTS = ["x", "adj", "L0_gnn_a_0", "L0_gnn_a_1", "L0_gnn_a_2", "L0_gnn_a_3", "L1_gnn_W", "L1_gnn_Wa",
          "L2_gnn_W", "L2_gnn_a_w", "L2_gnn_a_b", "L3_gnn_W", "L3_gnn_a1", "L3_gnn_a2"]


def kernel(**inputs):
    import concourse.bacc as bacc
    from concourse.bass_utils import run_bass_kernel_spmd

    nc = bacc.Bacc("TRN2", target_bir_lowering=False, num_devices=1)
    arrays, d = {}, {}
    for name in INPUTS:
        a = np.ascontiguousarray(inputs[name])
        arrays[f"in_{name}"] = a
        d[name] = nc.dram_tensor(f"in_{name}", a.shape, mybir.dt.from_np(a.dtype), kind="ExternalInput").ap()
    out = nc.dram_tensor("out_0", (BATCH, NODES, DIM), F32, kind="ExternalOutput").ap()
    build(nc, d["x"], d["adj"], [d[f"L0_gnn_a_{k}"] for k in range(KINDS)], d["L1_gnn_W"], d["L1_gnn_Wa"],
          d["L2_gnn_W"], d["L2_gnn_a_w"], d["L2_gnn_a_b"], d["L3_gnn_W"], d["L3_gnn_a1"], d["L3_gnn_a2"], out)
    r = run_bass_kernel_spmd(nc, [arrays], core_ids=[0])
    return r.results[0]["out_0"]
```

```python
from contextlib import ExitStack

import numpy as np
import concourse.bass as bass
from concourse import mybir

ALU = mybir.AluOpType
ACT = mybir.ActivationFunctionType
AX = mybir.AxisListType
F32 = mybir.dt.float32
BF16 = mybir.dt.bfloat16
I32 = mybir.dt.int32
U8 = mybir.dt.uint8

P = 128
BATCH, NODES, DIM = 16, 512, 128
TILES = NODES // P
KINDS = 4
H1, HID = 4, 32
H2 = 8
GROUP = 32
GROUPS = NODES // GROUP
PER_TILE = P // GROUP
WIN = NODES // 2 + GROUP
MIRROR = GROUPS // 2 - 1
MW = MIRROR * GROUP
ROUNDS = GROUP // 4
SPLIT = 96
NEG = -9.0e15
SLOPE0, SLOPE1, SLOPE2, SLOPE3 = 0.2, 0.2, 0.01, 0.2
EPS = 1e-5
BIG = 3.0e38


def lift(slope):
    return (1.0 - slope) / slope


SUMS = GROUPS * ROUNDS
ROW_ORDER = [*range(GROUPS // 2, GROUPS), *range(GROUPS // 2)]
LAST = SUMS + GROUPS + 4
TILE0 = [14 + 20 * t for t in range(TILES)]
ITEM2 = [9 + 9 * n // 4 for n in range(H2 * TILES)]
END2 = ITEM2[-1] + 8
LN3 = END2 + 4
ITEM3 = [LN3 + 9 + 3 * t for t in range(TILES)]
ITEM = ITEM2 + ITEM3
END3 = ITEM3[-1] + 10
USLOTS = 6
assert END3 < SUMS and TILE0[-1] + 18 < SUMS - 20

ACT_SHARE = 13
ON_ACT = [(r * ACT_SHARE) % GROUP < ACT_SHARE for r in range(GROUP)]


class Uses:
    def __init__(self, names):
        self.at = {name: n for n, name in enumerate(names)}

    def before(self, batch, name):
        return batch * len(self.at) + self.at[name]

    def upto(self, batch, name):
        return self.before(batch, name) + 1


EARLY_USES = Uses(["turn0"] + [f"{what}{t}" for t in range(TILES)
                               for what in [*(f"score{k}." for k in range(KINDS)), "pt", "attn"]]
                  + ["turn1", "yt", "vec"] + [f"yrot{v}" for v in range(PER_TILE)])
TURN_USES = Uses([f"{what}" for layer in (2, 3) for what in
                  [f"turn{layer}", f"ci{layer}", *(f"pt{layer}.{t}" for t in range(TILES))]])
VALUE_USES = Uses([f"{what}" for layer in (2, 3) for what in
                   [f"vec{layer}", f"proj{layer}", *(f"attn{layer}.{t}" for t in range(TILES))]])
ITEMS = len(ITEM)


def since(engine, semaphore, value):
    if not isinstance(value, int) or value > 0:
        engine.wait_ge(semaphore, value)


class Chain:
    def __init__(self, part):
        self.part = part
        self.slot = next(part, None)

    def run(self, slot):
        while self.slot is not None and self.slot <= slot:
            self.slot = next(self.part, None)


def build(nc, x, adj, a_k, w1, wa, w2, a_w, a_b, w3, a1, a2, out):
    with ExitStack() as ctx:
        def sb(name, shape, dt=F32):
            return ctx.enter_context(nc.sbuf_tensor(name, shape, dt))

        def sem(name):
            return ctx.enter_context(nc.semaphore(name))

        bank = [ctx.enter_context(nc.psum_tensor(f"bank{i}", [P, 512], F32)) for i in range(8)]

        ident = sb("ident", [P, P])
        ident_b = sb("ident_b", [P, P], BF16)
        spread = sb("spread", [P, PER_TILE, H1, GROUP], BF16)
        gather = sb("gather", [P, PER_TILE, P])
        reorder = sb("reorder", [P, P])
        head_block = sb("head_block", [P, H1, HID])
        pick = sb("pick", [SPLIT, H2, P], BF16)
        pick1 = sb("pick1", [SPLIT, H1, GROUP], BF16)
        half = sb("half", [P, TILES])

        ak_row = sb("ak_row", [P, KINDS])
        w1_sb = sb("w1_sb", [DIM, H1 * HID])
        w1t = sb("w1t", [H1 * HID, DIM])
        wa_block = sb("wa_block", [P, H1])
        slot_w = sb("slot_w", [P, ROUNDS, H1, ROUNDS])
        v1 = sb("v1", [DIM, SPLIT])
        w2_sb = sb("w2_sb", [DIM, DIM])
        w2t = sb("w2t", [DIM, DIM])
        aw_sb = sb("aw_sb", [H2, 2 * DIM])
        awt = sb("awt", [DIM, 2, H2])
        v2i = sb("v2i", [DIM, H2])
        v2j = sb("v2j", [DIM, SPLIT])
        b2_row = sb("b2_row", [P, H2])
        w3_sb = sb("w3_sb", [DIM, DIM])
        w3t = sb("w3t", [DIM, DIM])
        a12 = sb("a12", [DIM, 2])
        v3i = sb("v3i", [DIM, 1])
        v3j = sb("v3j", [DIM, SPLIT])

        adj_i = sb("adj_i", [P, TILES, NODES], I32)
        mask_1 = sb("mask_1", [P, TILES, NODES], BF16)
        mask_l = sb("mask_l", [P, TILES, NODES], BF16)
        mask_one = sb("mask_one", [P, TILES, NODES], BF16)
        is_kind = sb("is_kind", [P, KINDS - 1, TILES, NODES], U8)
        x_in = sb("x_in", [P, TILES, DIM])
        x_a = sb("x_a", [P, TILES, DIM])
        x_b = sb("x_b", [P, TILES, DIM])
        x_c = sb("x_c", [P, TILES, DIM])
        x_d = sb("x_d", [P, TILES, DIM])
        x_out = sb("x_out", [P, TILES, DIM])
        stats = [sb(f"stats{c}", [P, TILES, 6]) for c in "el"]
        mean_var = [sb(f"mean_var{c}", [P, TILES, 2]) for c in "el"]
        var_eps = [sb(f"var_eps{c}", [P, TILES]) for c in "el"]
        rstd = [sb(f"rstd{c}", [P, TILES]) for c in "el"]
        x_norm = [sb(f"x_norm{c}", [P, TILES, DIM]) for c in "el"]
        h_row = sb("h_row", [P, TILES, DIM])
        h_t0 = sb("h_t0", [P, NODES])
        h_t1 = sb("h_t1", [P, NODES + P])
        h_tl = sb("h_tl", [P, NODES])
        h_ak = sb("h_ak", [P, KINDS, NODES])
        score0 = sb("score0", [P, 2, NODES])
        relu0 = sb("relu0", [P, 2, NODES])
        nmax0 = sb("nmax0", [P, TILES]); rsum0 = sb("rsum0", [P, TILES]); rinv0 = sb("rinv0", [P, TILES])
        nmax1 = sb("nmax1", [P, GROUPS]); rsum1 = sb("rsum1", [P, GROUPS]); rinv1 = sb("rinv1", [P, GROUPS])
        nmaxl = sb("nmaxl", [P, ITEMS]); rsuml = sb("rsuml", [P, ITEMS]); rinvl = sb("rinvl", [P, ITEMS])
        y_t = sb("y_t", [P, NODES + WIN])
        y_rot = sb("y_rot", [P, PER_TILE, TILES, DIM])
        relu_s = sb("relu_s", [P, GROUP, WIN])
        d_raw = sb("d_raw", [P, 2, WIN])
        e1 = sb("e1", [P, GROUPS, NODES])
        p1 = sb("p1", [P, 2, NODES])
        p1_t = sb("p1_t", [P, 2, TILES, P])
        pe_t = sb("pe_t", [P, TILES, P])
        pl_t = sb("pl_t", [P, TILES, P])
        o1 = sb("o1", [P, 2, H1, HID])
        parts = [sb(f"parts{c}", [SPLIT, NODES], BF16) for c in "el"]
        part_r = [sb(f"part_r{c}", [SPLIT, NODES]) for c in "el"]
        part_m = [sb(f"part_m{c}", [SPLIT, NODES], BF16) for c in "el"]
        ci = sb("ci", [P, TILES, H2])
        hw = sb("hw", [P, TILES, DIM])
        ul = sb("ul", [P, USLOTS, NODES])
        acc2 = sb("acc2", [P, 2, NODES])
        elu_y = sb("elu_y", [P, TILES, DIM])
        elu_n = sb("elu_n", [P, TILES, DIM])

        w_in = sem("w_in")
        adj_in = sem("adj_in"); x_loaded = sem("x_loaded"); stored = sem("stored")
        adj_free = sem("adj_free")
        const_made = sem("const_made"); const_step = sem("const_step")
        prep_pe = sem("prep_pe"); prep_dve = sem("prep_dve"); table_in = sem("table_in")
        dve_passed = sem("dve_passed")
        step_e = sem("step_e"); step_l = sem("step_l"); step_m = sem("step_m")
        mask1_ready = sem("mask1_ready"); maskl_ready = sem("maskl_ready"); masks0_ready = sem("masks0_ready")
        stats_ready = [sem("stats_e"), sem("stats_l")]
        rstd_ready = [sem("rstd_e"), sem("rstd_l")]
        xn_ready = [sem("xn_e"), sem("xn_l")]
        early_ready = sem("early_ready"); early_free = sem("early_free")
        turn_ready = sem("turn_ready"); turn_free = sem("turn_free")
        value_ready = sem("value_ready"); value_free = sem("value_free")
        hak_ready = sem("hak_ready")
        relu0_ready = sem("relu0_ready"); max0_ready = sem("max0_ready"); exp0_ready = sem("exp0_ready")
        recip0_ready = sem("recip0_ready"); xb_ready = sem("xb_ready")
        parts1_ready = sem("parts1_ready")
        relu_act = sem("relu_act"); relu_dve = sem("relu_dve"); rounds_done = sem("rounds_done")
        raw_copied = sem("raw_copied"); mirrored = sem("mirrored"); ord_ready = sem("ord_ready"); ord_copied = sem("ord_copied")
        m1_ready = sem("m1_ready"); z1_ready = sem("z1_ready"); p1_ready = sem("p1_ready")
        p1t_ready = sem("p1t_ready"); p1t_act = sem("p1t_act"); p1t_dve = sem("p1t_dve")
        o1_ready = sem("o1_ready"); o1_recip = sem("o1_recip"); o1_scaled = sem("o1_scaled")
        x2_ready = sem("x2_ready"); xc_ready = sem("xc_ready")
        partsl_ready = sem("partsl_ready")
        z_ready = sem("z_ready"); relul_ready = sem("relul_ready"); maxl_ready = sem("maxl_ready")
        expl_ready = sem("expl_ready"); recipl_ready = sem("recipl_ready"); recip3_ready = sem("recip3_ready"); acc_ready = sem("acc_ready")
        elu_in = sem("elu_in"); elu_exp = sem("elu_exp"); x4_ready = sem("x4_ready")

        block = ctx.enter_context(nc.Block())

        spread_f = e1[:, 0, :]

        @block.sync
        def _(sp):
            def load(k):
                since(sp, early_free, EARLY_USES.upto(k - 1, "attn3"))
                sp.dma_start(x_in[:, :, :], x[bass.ds(k, 1), :, :].rearrange(
                    "o (t p) d -> p (o t) d", p=P)).then_inc(x_loaded, 16)
                since(sp, adj_free, k)
                sp.dma_start(adj_i[:, :, :], adj[bass.ds(k, 1), :, :].rearrange(
                    "o (t p) j -> p (o t) j", p=P)).then_inc(adj_in, 16)

            def store(k):
                sp.wait_ge(x4_ready, k + 1)
                sp.dma_start(out[bass.ds(k, 1), :, :].rearrange("o (t p) d -> p (o t) d", p=P),
                             x_out[:, :, :]).then_inc(stored, 16)

            load(0)
            for k in range(KINDS):
                sp.dma_start(ak_row[:, k:k + 1], a_k[k].rearrange("(d o) -> d o", o=1)).then_inc(w_in, 16)
            sp.dma_start(w1_sb[:, :], w1).then_inc(w_in, 16)
            sp.dma_start(w2_sb[:, :], w2).then_inc(w_in, 16)
            sp.dma_start(w3_sb[:, :], w3).then_inc(w_in, 16)
            sp.dma_start(aw_sb[:, :], a_w).then_inc(w_in, 16)
            sp.dma_start(b2_row[:, :], a_b.rearrange("(o h) -> o h", o=1).broadcast_to([P, H2])).then_inc(w_in, 16)
            sp.dma_start(a12[:, 0:1], a1.rearrange("(d o) -> d o", o=1)).then_inc(w_in, 16)
            sp.dma_start(a12[:, 1:2], a2.rearrange("(d o) -> d o", o=1)).then_inc(w_in, 16)
            sp.wait_ge(const_made, 1)
            for h in range(H1):
                sp.dma_start(wa_block[HID * h:HID * (h + 1), h:h + 1],
                             wa[h:h + 1, :].rearrange("o d -> d o")).then_inc(w_in, 16)
            load(1)
            with sp.Fori(2, BATCH) as k:
                load(k)
                store(k - 2)
            store(BATCH - 2)
            store(BATCH - 1)
            sp.wait_ge(stored, 16 * (BATCH + 1))

        W_LOADS = 16 * (KINDS + 7 + H1)
        CONST_MADE = 7

        @block.gpsimd
        def _(pool):
            g = nc.gpsimd
            g.memset(wa_block[:, :], 0.0).then_inc(const_made, 1)
            for t in (ident[:, :], ident_b[:, :], spread[:, :, :, :], reorder[:, :],
                      pick[:, :, :], pick1[:, :, :], head_block[:, :, :]):
                g.memset(t, 0.0).then_inc(const_step, 1)
            g.memset(half[:, :], -0.5).then_inc(const_made, 1)
            pool.wait_ge(const_step, 7)

            def one_where_zero(t, base, pattern):
                return g.affine_select(out=t, in_=t, compare_op=ALU.not_equal, fill=1.0, base=base,
                                       pattern=pattern, channel_multiplier=1)
            one_where_zero(ident[:, :], 0, [[-1, P]]).then_inc(const_made, 1)
            one_where_zero(ident_b[:, :], 0, [[-1, P]]).then_inc(const_made, 1)
            one_where_zero(spread[:, :, :, :], 0, [[-GROUP, PER_TILE], [0, H1], [-1, GROUP]]).then_inc(const_made, 1)
            one_where_zero(reorder[:, :].rearrange("p (h c s) -> p h c s", h=H1, c=4), 0,
                           [[-ROUNDS, H1], [-GROUP, 4], [-1, ROUNDS]]).then_inc(const_made, 1)
            for part in range(3):
                if part:
                    pool.wait_ge(const_step, 7 + 2 * part)
                one_where_zero(pick[:, :, :], -32 * part, [[-1, H2], [0, P]]).then_inc(const_step, 1)
                one_where_zero(pick1[:, :, :], -32 * part, [[-1, H1], [0, GROUP]]).then_inc(const_step, 1)
            pool.wait_ge(const_step, 13)
            g.memset(elu_n[:, 0, 0:1], 1.0).then_inc(const_made, 1)

            def rstd_of(late, k, n):
                pool.wait_ge(stats_ready[late], 2 * k + n + 1)
                g.tensor_tensor(rstd[late][:, :], var_eps[late][:, :], half[:, :],
                                ALU.pow).then_inc(rstd_ready[late], 1)

            def batch(b, late=True, early=True):
                if late:
                    rstd_of(1, b - 1, 0)
                if early:
                    rstd_of(0, b + 1, 0)
                if late:
                    rstd_of(1, b - 1, 1)
                if early:
                    rstd_of(0, b + 1, 1)

            batch(-1, late=False)
            batch(0, late=False)
            with pool.Fori(1, BATCH - 1) as b:
                batch(b)
            batch(BATCH - 1, early=False)
            batch(BATCH, early=False)

        @block.scalar
        def _(act):
            s = nc.scalar
            act.wait_ge(const_made, CONST_MADE)
            s.activation(elu_n[:, 0, 0:1], elu_n[:, 0, 0:1], ACT.Exp).then_inc(table_in, 1)

            def early(k):
                def use(name):
                    act.wait_ge(early_ready, EARLY_USES.upto(k, name))
                yield 11
                use("turn0")
                s.activation(h_t0[:, :], bank[7][:, :], ACT.Relu).then_inc(early_free, 1)
                for t in range(TILES):
                    yield TILE0[t] + 1
                    use(f"score0.{t}")
                    s.copy(score0[:, t % 2, :], bank[7][:, :]).then_inc(early_free, 1)
                    yield TILE0[t] + 11
                    act.wait_ge(early_free, EARLY_USES.upto(k, f"score{KINDS - 1}.{t}"))
                    s.activation(relu0[:, t % 2, :], score0[:, t % 2, :], ACT.Relu,
                                 scale=lift(SLOPE0)).then_inc(relu0_ready, 1)
                    yield TILE0[t] + 13
                    act.wait_ge(max0_ready, k * 4 + t + 1)
                    s.activation(score0[:, t % 2, :], score0[:, t % 2, :], ACT.Exp, scale=-1.0,
                                 bias=nmax0[:, t:t + 1], accum_out=rsum0[:, t:t + 1]).then_inc(exp0_ready, 1)
                    yield TILE0[t] + 15
                    use(f"pt{t}")
                    s.copy(pe_t[:, :, :].rearrange("p t i -> p (t i)"), bank[7][:, :]).then_inc(early_free, 1)
                yield TILE0[-1] + 24
                use("turn1")
                s.activation(h_t1[:, 0:NODES], bank[7][:, :], ACT.Relu)
                s.activation(h_t1[:, NODES:NODES + P], bank[7][:, 0:P], ACT.Relu).then_inc(early_free, 1)
                yield SUMS + 2
                use("yt")
                s.copy(y_t[:, 0:NODES], bank[7][:, :])
                s.copy(y_t[:, NODES:NODES + WIN], bank[7][:, 0:WIN]).then_inc(early_free, 1)

            def late(k):
                def turned(layer):
                    act.wait_ge(turn_ready, TURN_USES.upto(k, f"turn{layer}"))
                    s.activation(h_tl[:, :], bank[5][:, :], ACT.Relu).then_inc(turn_free, 1)

                def projected(layer):
                    act.wait_ge(value_ready, VALUE_USES.upto(k, f"proj{layer}"))
                    s.copy(hw[:, :, :].rearrange("p t d -> p (t d)"), bank[6][:, :]).then_inc(value_free, 1)

                def copy_pt(layer, t):
                    act.wait_ge(turn_ready, TURN_USES.upto(k, f"pt{layer}.{t}"))
                    s.copy(pl_t[:, :, :].rearrange("p t i -> p (t i)"), bank[5][:, :]).then_inc(turn_free, 1)

                def items(first, last):
                    for slot in range(ITEM[first] + 1, ITEM[last] + 11):
                        yield slot
                        for n in range(first, last + 1):
                            t, h = (n // H2, n % H2) if n < ITEMS - TILES else (n - ITEMS + TILES, 0)
                            slope = SLOPE2 if n < ITEMS - TILES else SLOPE3
                            if ITEM[n] + 1 == slot:
                                act.wait_ge(z_ready, k * ITEMS + n + 1)
                                if n == first:
                                    act.wait_ge(turn_free, TURN_USES.upto(k, "ci3" if n else "ci2"))
                                if n >= USLOTS:
                                    act.wait_ge(acc_ready, k * (ITEMS - TILES) + n - USLOTS + 1)
                                s.activation(ul[:, n % USLOTS, :], bank[3 + n % 2][:, :], ACT.Relu,
                                             bias=ci[:, t, h:h + 1], scale=lift(slope)).then_inc(relul_ready, 1)
                            if ITEM[n] + 4 == slot:
                                act.wait_ge(maxl_ready, k * ITEMS + n + 1)
                                s.activation(ul[:, n % USLOTS, :], ul[:, n % USLOTS, :], ACT.Exp, scale=-1.0,
                                             bias=nmaxl[:, n:n + 1],
                                             accum_out=rsuml[:, n:n + 1]).then_inc(expl_ready, 1)
                            if first == 0 and h == H2 - 1 and ITEM[n] + 9 == slot:
                                copy_pt(2, t)
                            if first and ITEM[n] + 7 == slot:
                                copy_pt(3, t)

                yield 4
                turned(2)
                yield 7
                projected(2)
                yield from items(0, ITEMS - TILES - 1)
                yield LN3 + 4
                turned(3)
                yield LN3 + 7
                projected(3)
                yield from items(ITEMS - TILES, ITEMS - 1)
                yield END3 + 2
                act.wait_ge(elu_in, k + 1)
                s.activation(elu_n[:, :, :], elu_n[:, :, :], ACT.Exp).then_inc(elu_exp, 1)

            def batch(b, has_late=True, has_early=True):
                chains = [Chain(late(b - 1))] * has_late + [Chain(early(b + 1))] * has_early

                def background(slot):
                    for chain in chains:
                        chain.run(slot)

                def copy_raw(q):
                    act.wait_ge(rounds_done, (b * GROUPS + q + 1) * ROUNDS)
                    since(act, ord_ready, b * GROUPS + q - 1)
                    s.copy(d_raw[:, q % 2, :], bank[q % 2][:, 0:WIN]).then_inc(raw_copied, 1)

                def copy_ord(q):
                    act.wait_ge(ord_ready, b * GROUPS + q + 1)
                    s.copy(e1[:, q, 0:WIN], bank[2][:, 0:WIN]).then_inc(ord_copied, 1)

                act.wait_ge(early_free, EARLY_USES.upto(b, "yt"))
                for slot in range(SUMS):
                    q, rnd = slot // ROUNDS, slot % ROUNDS
                    if True in ON_ACT[4 * rnd:4 * rnd + 4]:
                        since(act, rounds_done, (b * GROUPS + q - 1) * ROUNDS + rnd + 1)
                    for c in range(4):
                        if ON_ACT[4 * rnd + c]:
                            i = c * ROUNDS + rnd
                            s.activation(relu_s[:, i, :], y_t[:, q * GROUP:q * GROUP + WIN], ACT.Relu,
                                         bias=y_t[:, q * GROUP + i:q * GROUP + i + 1]).then_inc(relu_act, 1)
                    if rnd == 2 and q:
                        copy_raw(q - 1)
                    if rnd == 5 and q:
                        copy_ord(q - 1)
                    if 3 <= slot < 3 + 2 * PER_TILE and slot % 2:
                        v = (slot - 3) // 2
                        act.wait_ge(early_ready, EARLY_USES.upto(b, f"yrot{v}"))
                        s.copy(y_rot[:, v, :, :].rearrange("p t d -> p (t d)"), bank[7][:, :]).then_inc(early_free, 1)
                    background(slot)
                copy_raw(GROUPS - 1)
                for j in range(GROUPS + 1):
                    if j == 1:
                        copy_ord(GROUPS - 1)
                    if j < GROUPS:
                        act.wait_ge(z1_ready, b * GROUPS + j + 1)
                        since(act, p1t_ready, b * GROUPS + j - 1)
                        q = ROW_ORDER[j]
                        s.activation(p1[:, j % 2, :], e1[:, q, :], ACT.Exp, scale=-1.0,
                                     bias=nmax1[:, q:q + 1], accum_out=rsum1[:, q:q + 1]).then_inc(p1_ready, 1)
                    if j >= 1 and (j - 1) % 2 == 0:
                        act.wait_ge(p1t_ready, b * GROUPS + j)
                        since(act, o1_ready, b * GROUPS + j - 2)
                        s.copy(p1_t[:, 0, :, :].rearrange("p t i -> p (t i)"), bank[3][:, :]).then_inc(p1t_act, 1)
                    background(SUMS + j)
                background(LAST)

            def alone(part):
                Chain(part).run(LAST)

            alone(early(0))
            batch(0, has_late=False)
            with act.Fori(1, BATCH - 1) as b:
                batch(b)
            batch(BATCH - 1, has_early=False)
            alone(late(BATCH - 1))

        @block.vector
        def _(dve):
            v_ = nc.vector
            dve.sem_inc(stored, 16)
            dve.wait_ge(const_made, CONST_MADE)
            dve.wait_ge(w_in, W_LOADS)
            v_.memset(slot_w[:, :, :, :], 0.0).then_inc(prep_dve, 1)
            v_.memset(v1[:, :], 0.0).then_inc(prep_dve, 1)
            v_.memset(v2j[:, :], 0.0).then_inc(prep_dve, 1)
            v_.memset(v3j[:, :], 0.0).then_inc(prep_dve, 1)
            v_.tensor_copy(spread_f, spread[:, :, :, :].rearrange("p v h i -> p (v h i)")).then_inc(prep_dve, 1)
            dve.wait_ge(prep_dve, 5)
            for h in range(H1):
                v_.memset(head_block[HID * h:HID * (h + 1), h, :], 1.0).then_inc(prep_dve, 1)
            for k in range(ROUNDS):
                v_.tensor_scalar(slot_w[:, k, :, k], wa_block[:, :], 1.0 - SLOPE1, None, ALU.mult).then_inc(prep_dve, 1)
            dve.wait_ge(prep_pe, 1)
            v_.tensor_copy(w1t[:, :], bank[0][:, 0:P]).then_inc(prep_dve, 1)
            v_.tensor_copy(w2t[:, :], bank[0][:, P:2 * P]).then_inc(prep_dve, 1)
            v_.tensor_copy(w3t[:, :], bank[0][:, 2 * P:3 * P]).then_inc(prep_dve, 1)
            v_.tensor_copy(awt[:, :, :].rearrange("p a h -> p (a h)"), bank[1][:, 0:2 * H2]).then_inc(prep_dve, 1)
            v_.tensor_copy(gather[:, :, :].rearrange("p v i -> p (v i)"), bank[2][:, :]).then_inc(prep_dve, 1)
            dve.wait_ge(prep_pe, 2)
            for part in range(3):
                c = 32 * part
                v_.tensor_scalar(v1[:, c:c + H1], bank[3][:, 0:H1], SLOPE1, None, ALU.mult).then_inc(prep_dve, 1)
                v_.tensor_copy(v2j[:, c:c + H2], bank[3][:, 16:16 + H2]).then_inc(prep_dve, 1)
                v_.tensor_copy(v3j[:, c:c + 1], bank[3][:, 33:34]).then_inc(prep_dve, 1)
            v_.tensor_scalar(v2i[:, :], bank[3][:, 8:8 + H2], lift(SLOPE2), None, ALU.mult).then_inc(prep_dve, 1)
            v_.tensor_scalar(v3i[:, :], bank[3][:, 32:33], lift(SLOPE3), None, ALU.mult).then_inc(prep_dve, 1)
            v_.tensor_scalar(b2_row[:, :], b2_row[:, :], lift(SLOPE2), None, ALU.mult).then_inc(prep_dve, 1)
            dve.wait_ge(prep_dve, 9 + ROUNDS + 5 + 12)

            def leaky(to, lifted, u, slope, nmax):
                dve.sem_inc(dve_passed, 1)
                return v_.tensor_tensor_reduce(to, lifted, u, -slope, BIG, ALU.add, ALU.min, nmax)

            def own(semaphore, count, ins):
                ins.then_inc(semaphore, 1)
                dve.wait_ge(semaphore, count)

            STEPS_E, STEPS_L, STEPS_M = 4, 12, 3

            def layernorm_stats(which, src, semaphore, count):
                for t in range(TILES):
                    ins = v_.bn_stats(stats[which][:, t, :], src[:, t, :])
                own(semaphore, count, ins)
                dve.sem_inc(dve_passed, 1)
                for t in range(TILES):
                    ins = v_.bn_aggr(mean_var[which][:, t, :], stats[which][:, t, :])
                own(semaphore, count + 1, ins)
                v_.tensor_scalar(var_eps[which][:, :], mean_var[which][:, :, 1], EPS, None,
                                 ALU.add).then_inc(stats_ready[which], 1)

            def layernorm_apply(which, src, count):
                dve.wait_ge(rstd_ready[which], count)
                for t in range(TILES):
                    ins = v_.tensor_scalar(x_norm[which][:, t, :], src[:, t, :], mean_var[which][:, t, 0:1],
                                           rstd[which][:, t:t + 1], ALU.subtract, ALU.mult)
                ins.then_inc(xn_ready[which], 1)

            def split_high(which, src, semaphore, count):
                own(semaphore, count, v_.tensor_copy(parts[which][:, :], src))
                return v_.tensor_tensor(part_r[which][:, :], src, parts[which][:, :], ALU.subtract)

            def split_low(which, semaphore, count):
                own(semaphore, count, v_.tensor_copy(part_m[which][:, :], part_r[which][:, :]))
                v_.tensor_copy(parts[which][32:64, :], part_m[which][32:64, :])
                own(semaphore, count + 1, v_.tensor_tensor(part_r[which][:, :], part_r[which][:, :],
                                                           part_m[which][:, :], ALU.subtract))
                return v_.tensor_copy(parts[which][64:96, :], part_r[which][64:96, :])

            def early(k):
                yield 6
                dve.wait_ge(x_loaded, 16 * k + 16)
                layernorm_stats(0, x_in, step_e, k * STEPS_E + 1)
                yield 8
                layernorm_apply(0, x_in, 2 * k + 1)
                yield 9
                dve.wait_ge(xn_ready[0], 2 * k + 1)
                v_.tensor_scalar(h_row[:, :, :], x_norm[0][:, :, :], 0.0, None, ALU.max).then_inc(hak_ready, 1)
                yield 12
                dve.wait_ge(early_free, EARLY_USES.upto(k, "turn0"))
                for n in range(KINDS):
                    v_.tensor_scalar(h_ak[:, n, :], h_t0[:, :], ak_row[:, n:n + 1], None,
                                     ALU.mult).then_inc(hak_ready, 1)
                yield 13
                dve.wait_ge(adj_in, 16 * k + 16)
                v_.tensor_scalar(mask_one[:, :, :], adj_i[:, :, :], 1, NEG / SLOPE0, ALU.not_equal,
                                 ALU.mult).then_inc(masks0_ready, 1)
                for t in range(TILES):
                    for n in range(1, KINDS):
                        if t == 0:
                            yield TILE0[0] + 3 * n
                            v_.tensor_scalar(is_kind[:, n - 1, :, :], adj_i[:, :, :], n + 1, None,
                                             ALU.is_equal).then_inc(masks0_ready, 1)
                        yield TILE0[t] + 3 * n + 1
                        if t == 0:
                            dve.wait_ge(masks0_ready, k * KINDS + n + 1)
                        dve.wait_ge(early_free, EARLY_USES.upto(k, f"score{n - 1}.{t}"))
                        dve.wait_ge(early_ready, EARLY_USES.upto(k, f"score{n}.{t}"))
                        dve.sem_inc(dve_passed, 1)
                        v_.copy_predicated(score0[:, t % 2, :], is_kind[:, n - 1, t, :],
                                           bank[7][:, :]).then_inc(early_free, 1)
                    yield TILE0[t] + 12
                    dve.wait_ge(relu0_ready, k * 4 + t + 1)
                    leaky(score0[:, t % 2, :], relu0[:, t % 2, :], score0[:, t % 2, :], SLOPE0,
                          nmax0[:, t:t + 1]).then_inc(max0_ready, 1)
                    yield TILE0[t] + 16
                    dve.wait_ge(exp0_ready, k * 4 + t + 1)
                    v_.reciprocal(rinv0[:, t:t + 1], rsum0[:, t:t + 1]).then_inc(recip0_ready, 1)
                    yield TILE0[t] + 17
                    dve.wait_ge(recip0_ready, k * 4 + t + 1)
                    dve.wait_ge(early_ready, EARLY_USES.upto(k, f"attn{t}"))
                    if t == 0:
                        since(dve, xb_ready, k)
                    v_.scalar_tensor_tensor(x_a[:, t, :], bank[7][:, 0:P], rinv0[:, t:t + 1], x_in[:, t, :],
                                            ALU.mult, ALU.add).then_inc(early_free, 1)
                yield TILE0[-1] + 19
                dve.wait_ge(early_free, EARLY_USES.upto(k, "attn3"))
                layernorm_stats(0, x_a, step_e, k * STEPS_E + 3)
                yield TILE0[-1] + 21
                layernorm_apply(0, x_a, 2 * k + 2)

            def late(k):
                def vectors(layer):
                    base = k * STEPS_L + (0 if layer == 2 else 5)
                    yield (6 if layer == 2 else LN3 + 6)
                    dve.wait_ge(value_ready, VALUE_USES.upto(k, f"vec{layer}"))
                    ins = split_high(1, bank[6][0:SPLIT, :], step_l, base + 3)
                    ins.then_inc(value_free, 1)
                    dve.wait_ge(turn_ready, TURN_USES.upto(k, f"ci{layer}"))
                    if layer == 2:
                        v_.tensor_tensor(ci[:, :, :], bank[5][:, 0:TILES * H2].rearrange("p (t h) -> p t h", h=H2),
                                         b2_row[:, None, :].broadcast_to([P, TILES, H2]),
                                         ALU.add).then_inc(turn_free, 1)
                    else:
                        v_.tensor_copy(ci[:, :, 0], bank[5][:, 0:TILES]).then_inc(turn_free, 1)
                    yield (7 if layer == 2 else LN3 + 7)
                    dve.wait_ge(value_free, VALUE_USES.upto(k, f"vec{layer}"))
                    split_low(1, step_l, base + 4).then_inc(partsl_ready, 1)

                yield 0
                v_.tensor_copy(mask_l[:, :, :], mask_1[:, :, :]).then_inc(maskl_ready, 1)
                dve.wait_ge(xc_ready, k + 1)
                layernorm_stats(1, x_c, step_l, k * STEPS_L + 1)
                yield 2
                layernorm_apply(1, x_c, 2 * k + 1)
                yield from vectors(2)
                for slot in range(ITEM2[0] + 3, END2 + 5):
                    yield slot
                    for n in range(ITEMS - TILES):
                        t, h = n // H2, n % H2
                        u = ul[:, n % USLOTS, :]
                        at = acc2[:, t % 2, :]
                        if ITEM[n] + 3 == slot:
                            dve.wait_ge(relul_ready, k * ITEMS + n + 1)
                            leaky(u, u, bank[3 + n % 2][:, :], SLOPE2, nmaxl[:, n:n + 1]).then_inc(maxl_ready, 1)
                        if ITEM[n] + 6 == slot:
                            dve.wait_ge(expl_ready, k * ITEMS + n + 1)
                            v_.reciprocal(rinvl[:, n:n + 1], rsuml[:, n:n + 1]).then_inc(recipl_ready, 1)
                        if ITEM[n] + 7 == slot:
                            dve.wait_ge(recipl_ready, k * 32 + n + 1)
                            if h == 0:
                                if t >= 2:
                                    dve.wait_ge(turn_ready, TURN_USES.upto(k, f"pt2.{t - 2}"))
                                v_.tensor_scalar(at, u, rinvl[:, n:n + 1], None, ALU.mult).then_inc(acc_ready, 1)
                            else:
                                dve.wait_ge(acc_ready, k * (ITEMS - TILES) + n)
                                v_.scalar_tensor_tensor(at, u, rinvl[:, n:n + 1], at, ALU.mult,
                                                        ALU.add).then_inc(acc_ready, 1)
                        if h == H2 - 1 and ITEM[n] + 11 == slot:
                            dve.wait_ge(value_ready, VALUE_USES.upto(k, f"attn2.{t}"))
                            v_.scalar_tensor_tensor(x_d[:, t, :], bank[6][:, 0:P], 1.0 / H2, x_c[:, t, :],
                                                    ALU.mult, ALU.add).then_inc(value_free, 1)
                yield LN3
                dve.wait_ge(value_free, VALUE_USES.upto(k, "attn2.3"))
                layernorm_stats(1, x_d, step_l, k * STEPS_L + 6)
                yield LN3 + 2
                layernorm_apply(1, x_d, 2 * k + 2)
                yield from vectors(3)
                for slot in range(ITEM3[0] + 3, END3 + 1):
                    yield slot
                    for t in range(TILES):
                        n = ITEMS - TILES + t
                        u = ul[:, n % USLOTS, :]
                        if ITEM[n] + 3 == slot:
                            dve.wait_ge(relul_ready, k * ITEMS + n + 1)
                            leaky(u, u, bank[3 + n % 2][:, :], SLOPE3, nmaxl[:, n:n + 1]).then_inc(maxl_ready, 1)
                        if ITEM[n] + 8 == slot:
                            dve.wait_ge(expl_ready, k * ITEMS + n + 1)
                            v_.reciprocal(rinvl[:, n:n + 1], rsuml[:, n:n + 1]).then_inc(recip3_ready, 1)
                        if ITEM[n] + 9 == slot:
                            dve.wait_ge(recip3_ready, k * 4 + t + 1)
                            dve.wait_ge(value_ready, VALUE_USES.upto(k, f"attn3.{t}"))
                            v_.tensor_scalar(elu_y[:, t, :], bank[6][:, 0:P], rinvl[:, n:n + 1], None,
                                             ALU.mult).then_inc(value_free, 1)
                yield END3 + 1
                dve.wait_ge(value_free, VALUE_USES.upto(k, "attn3.3"))
                v_.tensor_scalar(elu_n[:, :, :], elu_y[:, :, :], 0.0, None, ALU.min).then_inc(elu_in, 1)
                own(step_l, k * STEPS_L + 11, v_.tensor_scalar(elu_y[:, :, :], elu_y[:, :, :], 0.0, -1.0,
                                                               ALU.max, ALU.add))
                yield END3 + 3
                dve.wait_ge(elu_exp, k + 1)
                own(step_l, k * STEPS_L + 12, v_.tensor_tensor(elu_y[:, :, :], elu_y[:, :, :], elu_n[:, :, :],
                                                               ALU.add))
                dve.wait_ge(stored, 16 * k + 16)
                v_.tensor_tensor(x_out[:, :, :], elu_y[:, :, :], x_d[:, :, :], ALU.add).then_inc(x4_ready, 1)

            def batch(b, has_late=True, has_early=True):
                chains = [Chain(late(b - 1))] * has_late + [Chain(early(b + 1))] * has_early

                def background(slot):
                    for chain in chains:
                        chain.run(slot)

                def mirror(q):
                    dve.wait_ge(ord_copied, b * GROUPS + q + 1)
                    flat = e1[:, :, :].rearrange("p q j -> p (q j)")
                    inside = min(MIRROR, GROUPS - 1 - q)
                    for first, count, row in ((1, inside, q + 1), (inside + 1, MIRROR - inside, q + inside + 1 - GROUPS)):
                        if count:
                            at = row * NODES + NODES - GROUP * first
                            stride = NODES - GROUP
                            ins = v_.transpose(blocks(flat, at, count, stride),
                                               e1[:, q, GROUP * first:GROUP * (first + count)].rearrange(
                                                   "p (m c) -> p m c", c=GROUP))
                    ins.then_inc(mirrored, 1)

                def blocks(flat, at, count, stride):
                    if at + count * stride <= GROUPS * NODES:
                        return flat[:, at:at + count * stride].rearrange("p (m c) -> p m c", c=stride)[:, :, 0:GROUP]
                    at -= stride - GROUP
                    return flat[:, at:at + count * stride].rearrange("p (m c) -> p m c", c=stride)[
                        :, :, stride - GROUP:stride]

                dve.wait_ge(early_free, EARLY_USES.upto(b, "yt"))
                for slot in range(SUMS):
                    q, rnd = slot // ROUNDS, slot % ROUNDS
                    if slot == 1:
                        if has_late:
                            dve.wait_ge(maskl_ready, b)
                        v_.tensor_scalar(mask_1[:, :, :], adj_i[:, :, :], 0, NEG, ALU.is_le,
                                         ALU.mult).then_inc(adj_free, 1)
                        dve.wait_ge(early_free, EARLY_USES.upto(b, "attn3"))
                        v_.tensor_copy(x_b[:, :, :], x_a[:, :, :]).then_inc(xb_ready, 1)
                    if slot == 2:
                        dve.wait_ge(early_ready, EARLY_USES.upto(b, "vec"))
                        split_high(0, bank[7][0:SPLIT, :], step_m, b * STEPS_M + 1).then_inc(early_free, 1)
                    if slot == 3:
                        dve.wait_ge(early_free, EARLY_USES.upto(b, "vec"))
                        split_low(0, step_m, b * STEPS_M + 2).then_inc(parts1_ready, 1)
                    since(dve, rounds_done, (b * GROUPS + q - 1) * ROUNDS + rnd + 1)
                    for c in range(4):
                        if not ON_ACT[4 * rnd + c]:
                            i = c * ROUNDS + rnd
                            v_.tensor_scalar(relu_s[:, i, :], y_t[:, q * GROUP:q * GROUP + WIN],
                                             y_t[:, q * GROUP + i:q * GROUP + i + 1], 0.0, ALU.add,
                                             ALU.max).then_inc(relu_dve, 1)
                    if rnd == 7 and q:
                        mirror(q - 1)
                    background(slot)
                for j in range(GROUPS + 3):
                    if j == 2:
                        mirror(GROUPS - 1)
                    if j < GROUPS:
                        q = ROW_ORDER[j]
                        dve.wait_ge(mirrored, b * GROUPS + (q if q >= GROUPS // 2 else GROUPS))
                        dve.wait_ge(m1_ready, b * GROUPS + j + 1)
                        dve.sem_inc(dve_passed, 1)
                        v_.tensor_tensor_reduce(e1[:, q, :], e1[:, q, :], bank[j % 2][:, :], -1.0, BIG, ALU.add,
                                                ALU.min, nmax1[:, q:q + 1]).then_inc(z1_ready, 1)
                    if 2 <= j < GROUPS + 2 and j % 2 == 1:
                        n = j - 2
                        dve.wait_ge(p1t_ready, b * GROUPS + n + 1)
                        since(dve, o1_ready, b * GROUPS + n - 1)
                        v_.tensor_copy(p1_t[:, 1, :, :].rearrange("p t i -> p (t i)"),
                                       bank[5][:, :]).then_inc(p1t_dve, 1)
                    if j >= 3:
                        n = j - 3
                        q = ROW_ORDER[n]
                        dve.wait_ge(p1_ready, b * GROUPS + n + 1)
                        v_.reciprocal(rinv1[:, q:q + 1], rsum1[:, q:q + 1]).then_inc(o1_recip, 1)
                        dve.wait_ge(o1_recip, b * GROUPS + n + 1)
                        dve.wait_ge(o1_ready, b * GROUPS + n + 1)
                        since(dve, x2_ready, b * GROUPS + n - 1)
                        v_.scalar_tensor_tensor(o1[:, n % 2, :, :].rearrange("p h d -> p (h d)"),
                                                bank[(4, 6)[n % 2]][:, 0:P], rinv1[:, q:q + 1],
                                                head_block[:, :, :].rearrange("p h d -> p (h d)"),
                                                ALU.mult, ALU.mult).then_inc(o1_scaled, 1)
                    background(SUMS + j)
                background(LAST)
                dve.wait_ge(x2_ready, b * GROUPS + GROUPS)
                dve.wait_ge(xb_ready, b + 1)
                v_.tensor_tensor(x_c[:, :, :].rearrange("p t d -> p (t d)"), bank[2][:, :],
                                 x_b[:, :, :].rearrange("p t d -> p (t d)"), ALU.add).then_inc(xc_ready, 1)

            def alone(part):
                Chain(part).run(LAST)

            alone(early(0))
            batch(0, has_late=False)
            with dve.Fori(1, BATCH - 1) as b:
                batch(b)
            batch(BATCH - 1, has_early=False)
            alone(late(BATCH - 1))

        @block.tensor
        def _(pe):
            T = nc.tensor

            def mm(o, l, r, start=True, stop=True):
                return T.matmul(o, l, r, start=start, stop=stop, skip_group_check=True)

            pe.wait_ge(const_made, CONST_MADE)
            pe.wait_ge(w_in, W_LOADS)
            pe.wait_ge(prep_dve, 5)
            for n, w in enumerate((w1_sb, w2_sb, w3_sb)):
                T.transpose(bank[0][:, n * P:(n + 1) * P], w[:, :], ident[:, :])
            for n in range(2):
                T.transpose(bank[1][:, n * H2:(n + 1) * H2], aw_sb[:, n * DIM:(n + 1) * DIM], ident[0:H2, 0:H2])
            for v in range(PER_TILE):
                ins = T.transpose(bank[2][:, v * P:(v + 1) * P], spread_f[:, v * P:(v + 1) * P], ident[:, :])
            ins.then_inc(prep_pe, 1)
            pe.wait_ge(prep_dve, 9 + ROUNDS + 5)
            mm(bank[3][:, 0:H1], w1t[:, :], wa_block[:, :])
            mm(bank[3][:, 8:8 + H2], w2t[:, :], awt[:, 0, :])
            mm(bank[3][:, 16:16 + H2], w2t[:, :], awt[:, 1, :])
            mm(bank[3][:, 32:34], w3_sb[:, :], a12[:, :]).then_inc(prep_pe, 1)
            pe.wait_ge(prep_dve, 9 + ROUNDS + 5 + 12)

            def turn(to, src):
                for t in range(TILES):
                    ins = T.transpose(to[:, t * P:(t + 1) * P], src[:, t * P:(t + 1) * P], ident[:, :])
                return ins

            def rows(t3):
                return t3.rearrange("p t d -> p (t d)")

            def attend(to, weights, values):
                for t in range(TILES):
                    ins = mm(to, weights[:, t, :], values[:, t, :], t == 0, t == TILES - 1)
                return ins

            def early(k):
                def free(name):
                    since(pe, early_free, EARLY_USES.before(k, name))

                yield 10
                pe.wait_ge(xn_ready[0], 2 * k + 1)
                free("turn0")
                turn(bank[7], rows(x_norm[0][:, :, :])).then_inc(early_ready, 1)
                for t in range(TILES):
                    for n in range(KINDS):
                        yield TILE0[t] + 3 * n
                        pe.wait_ge(hak_ready, k * 5 + 1 + n + 1)
                        if n == 0:
                            pe.wait_ge(masks0_ready, k * KINDS + 1)
                        free(f"score{n}.{t}")
                        ins = mm(bank[7][:, :], h_ak[:, n, t * P:(t + 1) * P], h_t0[:, :], True, n > 0)
                        if n == 0:
                            ins = mm(bank[7][:, :], ident_b[:, :], mask_one[:, t, :], False, True)
                        ins.then_inc(early_ready, 1)
                    yield TILE0[t] + 14
                    pe.wait_ge(exp0_ready, k * 4 + t + 1)
                    free(f"pt{t}")
                    turn(bank[7], score0[:, t % 2, :]).then_inc(early_ready, 1)
                    yield TILE0[t] + 16
                    free(f"attn{t}")
                    attend(bank[7][:, 0:P], pe_t, h_row).then_inc(early_ready, 1)
                yield TILE0[-1] + 23
                pe.wait_ge(xn_ready[0], 2 * k + 2)
                free("turn1")
                turn(bank[7], rows(x_norm[0][:, :, :])).then_inc(early_ready, 1)
                yield SUMS + 1
                free("yt")
                mm(bank[7][:, :], w1_sb[:, :], h_t1[:, 0:NODES]).then_inc(early_ready, 1)

            def late(k):
                def turn_free_of(name):
                    since(pe, turn_free, TURN_USES.before(k, name))

                def value_free_of(name):
                    since(pe, value_free, VALUE_USES.before(k, name))

                def front(layer, vj, vi, width, w):
                    n = layer - 2
                    at = 3 if layer == 2 else LN3 + 3
                    yield at
                    pe.wait_ge(xn_ready[1], 2 * k + n + 1)
                    if layer == 3:
                        turn_free_of("turn3")
                    turn(bank[5], rows(x_norm[1][:, :, :])).then_inc(turn_ready, 1)
                    yield at + 2
                    pe.wait_ge(turn_free, TURN_USES.upto(k, f"turn{layer}"))
                    if layer == 3:
                        value_free_of("vec3")
                    mm(bank[6][0:SPLIT, :], vj, h_tl[:, :]).then_inc(value_ready, 1)
                    for t in range(TILES):
                        ins = mm(bank[5][:, t * width:(t + 1) * width], h_tl[:, t * P:(t + 1) * P], vi)
                    ins.then_inc(turn_ready, 1)
                    yield at + 3
                    value_free_of(f"proj{layer}")
                    for t in range(TILES):
                        ins = mm(bank[6][:, t * P:(t + 1) * P], h_tl[:, t * P:(t + 1) * P], w)
                    ins.then_inc(value_ready, 1)

                def scores(n, t, h):
                    if n >= 2:
                        pe.wait_ge(maxl_ready, k * ITEMS + n - 1)
                    mm(bank[3 + n % 2][:, :], pick[:, h, :], parts[1][:, :], True, False)
                    mm(bank[3 + n % 2][:, :], ident_b[:, :], mask_l[:, t, :], False, True).then_inc(z_ready, 1)

                yield from front(2, v2j[:, :], v2i[:, :], H2, w2_sb[:, :])
                for slot in range(ITEM2[0], END2 + 4):
                    yield slot
                    for n in range(ITEMS - TILES):
                        t, h = n // H2, n % H2
                        if ITEM[n] == slot:
                            if n == 0:
                                pe.wait_ge(partsl_ready, 2 * k + 1)
                                pe.wait_ge(maskl_ready, k + 1)
                            scores(n, t, h)
                        if h == H2 - 1 and ITEM[n] + 8 == slot:
                            pe.wait_ge(acc_ready, k * (ITEMS - TILES) + n + 1)
                            turn_free_of(f"pt2.{t}")
                            turn(bank[5], acc2[:, t % 2, :]).then_inc(turn_ready, 1)
                        if h == H2 - 1 and ITEM[n] + 10 == slot:
                            pe.wait_ge(turn_free, TURN_USES.upto(k, f"pt2.{t}"))
                            value_free_of(f"attn2.{t}")
                            attend(bank[6][:, 0:P], pl_t, hw).then_inc(value_ready, 1)
                yield from front(3, v3j[:, :], v3i[:, :], 1, w3t[:, :])
                for slot in range(ITEM3[0], END3):
                    yield slot
                    for t in range(TILES):
                        n = ITEMS - TILES + t
                        if ITEM[n] == slot:
                            if t == 0:
                                pe.wait_ge(partsl_ready, 2 * k + 2)
                            scores(n, t, 0)
                        if ITEM[n] + 6 == slot:
                            pe.wait_ge(expl_ready, k * ITEMS + n + 1)
                            turn_free_of(f"pt3.{t}")
                            turn(bank[5], ul[:, n % USLOTS, :]).then_inc(turn_ready, 1)
                        if ITEM[n] + 8 == slot:
                            pe.wait_ge(turn_free, TURN_USES.upto(k, f"pt3.{t}"))
                            value_free_of(f"attn3.{t}")
                            attend(bank[6][:, 0:P], pl_t, hw).then_inc(value_ready, 1)

            def batch(b, has_late=True, has_early=True):
                chains = [Chain(late(b - 1))] * has_late + [Chain(early(b + 1))] * has_early

                def background(slot):
                    for chain in chains:
                        chain.run(slot)

                def put_in_order(q):
                    pe.wait_ge(raw_copied, b * GROUPS + q + 1)
                    since(pe, ord_copied, b * GROUPS + q)
                    if q == 0:
                        since(pe, xc_ready, b)
                    mm(bank[2][:, 0:WIN], reorder[:, :], d_raw[:, q % 2, :]).then_inc(ord_ready, 1)

                for slot in range(SUMS):
                    q, rnd = slot // ROUNDS, slot % ROUNDS
                    if rnd == 0:
                        if q >= 2:
                            pe.wait_ge(raw_copied, b * GROUPS + q - 1)
                        elif q == 0:
                            since(pe, z1_ready, b * GROUPS)
                    on_act = sum(ON_ACT[0:4 * rnd + 4])
                    since(pe, relu_act, (b * GROUPS + q) * ACT_SHARE + on_act)
                    since(pe, relu_dve, (b * GROUPS + q) * (GROUP - ACT_SHARE) + 4 * rnd + 4 - on_act)
                    for c in range(4):
                        ins = mm(bank[q % 2][32 * c:32 * c + 32, 0:WIN],
                                 slot_w[:, rnd, :, :].rearrange("p h s -> p (h s)"),
                                 relu_s[:, c * ROUNDS + rnd, :], rnd == 0, rnd == ROUNDS - 1)
                    ins.then_inc(rounds_done, 1)
                    if slot == 0:
                        since(pe, early_free, EARLY_USES.before(b, "vec"))
                        mm(bank[7][0:SPLIT, :], v1[:, :], h_t1[:, 0:NODES]).then_inc(early_ready, 1)
                    if 2 <= slot < 2 + 2 * PER_TILE and slot % 2 == 0:
                        v = (slot - 2) // 2
                        since(pe, early_free, EARLY_USES.before(b, f"yrot{v}"))
                        for t in range(TILES):
                            at = v * GROUP + t * P
                            ins = mm(bank[7][:, t * P:(t + 1) * P], h_t1[:, at:at + P], w1_sb[:, :])
                        ins.then_inc(early_ready, 1)
                    if rnd == 3 and q:
                        put_in_order(q - 1)
                    background(slot)
                put_in_order(GROUPS - 1)
                if has_late:
                    pe.wait_ge(maxl_ready, b * ITEMS)
                    pe.wait_ge(turn_free, TURN_USES.upto(b - 1, "pt3.3"))
                    pe.wait_ge(value_free, VALUE_USES.upto(b - 1, "attn3.3"))
                pe.wait_ge(parts1_ready, b + 1)
                pe.wait_ge(adj_free, b + 1)
                for j in range(GROUPS + 3):
                    if j < GROUPS:
                        q = ROW_ORDER[j]
                        if j >= 2:
                            pe.wait_ge(z1_ready, b * GROUPS + j - 1)
                        at = q * GROUP
                        head = NODES - at
                        lhs = spread[:, q % PER_TILE, :, :].rearrange("p h i -> p (h i)")
                        picked = pick1[:, :, :].rearrange("p h i -> p (h i)")
                        mask = mask_1[:, q // PER_TILE, :]
                        to = bank[j % 2]
                        mm(to[:, 0:head], lhs, mask[:, at:NODES], True, False)
                        if at:
                            mm(to[:, head:NODES], lhs, mask[:, 0:at], False, False)
                        ins = mm(to[:, 0:head], picked, parts[0][:, at:NODES], False, True)
                        if at:
                            ins = mm(to[:, head:NODES], picked, parts[0][:, 0:at], False, True)
                        ins.then_inc(m1_ready, 1)
                    if 1 <= j <= GROUPS:
                        n = j - 1
                        pe.wait_ge(p1_ready, b * GROUPS + n + 1)
                        if n >= 2:
                            pe.wait_ge((p1t_act, p1t_dve)[n % 2], b * 8 + n // 2)
                        turn(bank[(3, 5)[n % 2]], p1[:, n % 2, :]).then_inc(p1t_ready, 1)
                    if 2 <= j <= GROUPS + 1:
                        n = j - 2
                        q = ROW_ORDER[n]
                        pe.wait_ge((p1t_act, p1t_dve)[n % 2], b * 8 + n // 2 + 1)
                        if n >= 2:
                            pe.wait_ge(o1_scaled, b * GROUPS + n - 1)
                        for t in range(TILES):
                            ins = mm(bank[(4, 6)[n % 2]][:, 0:P], p1_t[:, n % 2, t, :],
                                     y_rot[:, q % PER_TILE, (q // PER_TILE + t) % TILES, :], t == 0, t == TILES - 1)
                        ins.then_inc(o1_ready, 1)
                    if j >= 3:
                        n = j - 3
                        q = ROW_ORDER[n]
                        pe.wait_ge(o1_scaled, b * GROUPS + n + 1)
                        if n == 0:
                            pe.wait_ge(ord_copied, b * GROUPS + GROUPS)
                        tile = q // PER_TILE
                        mm(bank[2][:, tile * P:(tile + 1) * P], gather[:, q % PER_TILE, :],
                           o1[:, n % 2, :, :].rearrange("p h d -> p (h d)"), q % PER_TILE == 0,
                           q % PER_TILE == PER_TILE - 1).then_inc(x2_ready, 1)
                    background(SUMS + j)
                background(LAST)

            def alone(part):
                Chain(part).run(LAST)

            alone(early(0))
            batch(0, has_late=False)
            with pe.Fori(1, BATCH - 1) as b:
                batch(b)
            batch(BATCH - 1, has_early=False)
            alone(late(BATCH - 1))


INPUTS = ["x", "adj", "L0_gnn_a_0", "L0_gnn_a_1", "L0_gnn_a_2", "L0_gnn_a_3", "L1_gnn_W", "L1_gnn_Wa",
          "L2_gnn_W", "L2_gnn_a_w", "L2_gnn_a_b", "L3_gnn_W", "L3_gnn_a1", "L3_gnn_a2"]


def kernel(**inputs):
    import concourse.bacc as bacc
    from concourse.bass_utils import run_bass_kernel_spmd

    nc = bacc.Bacc("TRN2", target_bir_lowering=False, num_devices=1)
    arrays, d = {}, {}
    for name in INPUTS:
        a = np.ascontiguousarray(inputs[name])
        arrays[f"in_{name}"] = a
        d[name] = nc.dram_tensor(f"in_{name}", a.shape, mybir.dt.from_np(a.dtype), kind="ExternalInput").ap()
    out = nc.dram_tensor("out_0", (BATCH, NODES, DIM), F32, kind="ExternalOutput").ap()
    build(nc, d["x"], d["adj"], [d[f"L0_gnn_a_{k}"] for k in range(KINDS)], d["L1_gnn_W"], d["L1_gnn_Wa"],
          d["L2_gnn_W"], d["L2_gnn_a_w"], d["L2_gnn_a_b"], d["L3_gnn_W"], d["L3_gnn_a1"], d["L3_gnn_a2"], out)
    r = run_bass_kernel_spmd(nc, [arrays], core_ids=[0])
    return r.results[0]["out_0"]
```

```python
from contextlib import ExitStack

import numpy as np
import concourse.bass as bass
from concourse import mybir

ALU = mybir.AluOpType
ACT = mybir.ActivationFunctionType
F32 = mybir.dt.float32
BF16 = mybir.dt.bfloat16
I32 = mybir.dt.int32
U8 = mybir.dt.uint8

P = 128
BATCH, NODES, DIM = 16, 512, 128
TILES = NODES // P
KINDS = 4
H1, HID = 4, 32
H2 = 8
GROUP = 32
GROUPS = NODES // GROUP
PER_TILE = P // GROUP
WIN = NODES // 2 + GROUP
WINS = [WIN if q < GROUPS // 2 else WIN - GROUP for q in range(GROUPS)]
ROUNDS = GROUP // 4
SPLIT = 96
NEG = -9.0e15
SLOPE0, SLOPE1, SLOPE2, SLOPE3 = 0.2, 0.2, 0.01, 0.2
EPS = 1e-5
BIG = 3.0e38


def lift(slope):
    return (1.0 - slope) / slope


SUMS = GROUPS * ROUNDS
ROW_ORDER = [*range(GROUPS // 2, GROUPS), *range(GROUPS // 2)]
LAST = SUMS + GROUPS
EXTRA = {3: "vec", 5: "yrot0", 7: "yrot1", 9: "yrot2", 11: "yrot3"}
LN0 = SUMS - 7
TILE0 = [7 + 24 * t for t in range(TILES)]
LN1 = TILE0[-1] + 24
LN = {2: 3, 3: 109}
TURNED, RELUED, SOURCED, SPLITTED = {2: 8, 3: 6}, {2: 10, 3: 8}, {2: 11, 3: 9}, {2: 13, 3: 11}
ITEM2 = [LN[2] + 20 + 9 * n // 4 for n in range(H2 * TILES)]
ITEM3 = [LN[3] + 19 + 2 * t for t in range(TILES)]
ITEM = ITEM2 + ITEM3
RELU, LEAKY, EXP, SUM = {2: 1, 3: 1}, {2: 3, 3: 2}, {2: 5, 3: 3}, {2: 8}
TURN, COPY, ATTEND, ADD = {2: 10, 3: 4}, {2: 12, 3: 5}, {2: 13, 3: 6}, {2: 15, 3: 7}
END = {2: ITEM2[-1] + ADD[2], 3: ITEM3[-1] + ADD[3]}
USLOTS = 6
LEAD = 5
RELU_ROW = GROUPS - LEAD - 2
assert LN1 + 8 < SUMS and END[2] < LN[3] and END[3] + 2 < LAST

ACT_SHARE = 13
ON_ACT = [(r * ACT_SHARE) % GROUP < ACT_SHARE for r in range(GROUP)]


class Uses:
    def __init__(self, names):
        self.at = {name: n for n, name in enumerate(names)}

    def before(self, batch, name):
        return batch * len(self.at) + self.at[name]

    def upto(self, batch, name):
        return self.before(batch, name) + 1


EARLY_USES = Uses(["turn0"] + [f"{what}{t}" for t in range(TILES)
                               for what in [*(f"score{k}." for k in range(KINDS)), "pt", "attn"]]
                  + ["turn1", "yt"])
ORD_USES = Uses([name for q in range(GROUPS) for name in
                 ([EXTRA[q + 1]] if q + 1 in EXTRA else []) + [f"ord{q}"]])
TURN_USES = Uses([what for layer in (2, 3) for what in
                  [f"turn{layer}", f"ci{layer}", *(f"pt{layer}.{t}" for t in range(TILES))]])
VALUE_USES = Uses([what for layer in (2, 3) for what in
                   [f"vec{layer}", f"proj{layer}", *(f"attn{layer}.{t}" for t in range(TILES))]])
ITEMS = len(ITEM)


FIRST_BANKS = (7, 6, 5, 4)


def zbank(n):
    return 3 + n % 2 if n < len(ITEM2) else 4


def since(engine, semaphore, value):
    if not isinstance(value, int) or value > 0:
        engine.wait_ge(semaphore, value)


class Chain:
    def __init__(self, part):
        self.part = part
        self.slot = next(part, None)

    def run(self, slot):
        while self.slot is not None and self.slot <= slot:
            self.slot = next(self.part, None)


def build(nc, x, adj, a_k, w1, wa, w2, a_w, a_b, w3, a1, a2, out):
    with ExitStack() as ctx:
        def sb(name, shape, dt=F32):
            return ctx.enter_context(nc.sbuf_tensor(name, shape, dt))

        def sem(name):
            return ctx.enter_context(nc.semaphore(name))

        bank = [ctx.enter_context(nc.psum_tensor(f"bank{i}", [P, 512], F32)) for i in range(8)]

        ident = sb("ident", [P, P])
        ident_b = sb("ident_b", [P, P], BF16)
        far_b = sb("far_b", [P, P], BF16)
        spread = sb("spread", [P, PER_TILE, H1, GROUP], BF16)
        gather = sb("gather", [P, PER_TILE, P])
        reorder = sb("reorder", [P, P])
        head_block = sb("head_block", [P, H1, HID])
        pick = sb("pick", [SPLIT, H2, P], BF16)
        pick1 = sb("pick1", [SPLIT, H1, GROUP], BF16)
        half = sb("half", [P, TILES])

        ak_row = sb("ak_row", [P, KINDS])
        w1_sb = sb("w1_sb", [DIM, H1 * HID])
        w1t = sb("w1t", [H1 * HID, DIM])
        wa_block = sb("wa_block", [P, H1])
        slot_w = sb("slot_w", [P, ROUNDS, H1, ROUNDS])
        v1 = sb("v1", [DIM, SPLIT])
        w2_sb = sb("w2_sb", [DIM, DIM])
        w2t = sb("w2t", [DIM, DIM])
        aw_sb = sb("aw_sb", [H2, 2 * DIM])
        awt = sb("awt", [DIM, 2, H2])
        v2i = sb("v2i", [DIM, H2])
        v2j = sb("v2j", [DIM, SPLIT])
        b2_row = sb("b2_row", [P, H2])
        w3_sb = sb("w3_sb", [DIM, DIM])
        w3t = sb("w3t", [DIM, DIM])
        a12 = sb("a12", [DIM, 2])
        v3i = sb("v3i", [DIM, 1])
        v3j = sb("v3j", [DIM, SPLIT])

        adj_i = sb("adj_i", [P, TILES, NODES], I32)
        mask_1 = sb("mask_1", [P, TILES, NODES], BF16)
        mask_n = sb("mask_n", [P, TILES, NODES], BF16)
        mask_l = sb("mask_l", [P, TILES, NODES], BF16)
        mask_one = sb("mask_one", [P, TILES, NODES], BF16)
        is_kind = sb("is_kind", [P, KINDS - 1, TILES, NODES], U8)
        x_in = sb("x_in", [P, TILES, DIM])
        x_a = sb("x_a", [P, TILES, DIM])
        x_b = sb("x_b", [P, TILES, DIM])
        x_c = sb("x_c", [P, TILES, DIM])
        x_d = sb("x_d", [P, TILES, DIM])
        x_out = sb("x_out", [P, TILES, DIM])
        stats = [sb(f"stats{c}", [P, TILES, 6]) for c in "el"]
        mean_var = [sb(f"mean_var{c}", [P, TILES, 2]) for c in "el"]
        var_eps = [sb(f"var_eps{c}", [P, TILES]) for c in "el"]
        rstd = [sb(f"rstd{c}", [P, TILES]) for c in "el"]
        x_norm = [sb(f"x_norm{c}", [P, TILES, DIM]) for c in "el"]
        h_row = sb("h_row", [P, TILES, DIM])
        h_t0 = sb("h_t0", [P, NODES])
        h_t1 = sb("h_t1", [P, NODES + P])
        h_tl = sb("h_tl", [P, NODES])
        h_ak = sb("h_ak", [P, KINDS, NODES])
        score0 = sb("score0", [P, 2, NODES])
        relu0 = sb("relu0", [P, 2, NODES])
        nmax0 = sb("nmax0", [P, TILES]); rsum0 = sb("rsum0", [P, TILES]); rinv0 = sb("rinv0", [P, TILES])
        nmax1 = sb("nmax1", [P, GROUPS]); rsum1 = sb("rsum1", [P, GROUPS]); rinv1 = sb("rinv1", [P, GROUPS])
        nmaxl = sb("nmaxl", [P, ITEMS]); rsuml = sb("rsuml", [P, ITEMS]); rinvl = sb("rinvl", [P, ITEMS])
        y_t = sb("y_t", [P, NODES + WIN])
        y_rot = sb("y_rot", [P, PER_TILE, TILES, DIM])
        relu_s = sb("relu_s", [P, GROUP, WIN])
        d_raw = sb("d_raw", [P, 2, WIN])
        e1 = sb("e1", [P, GROUPS, NODES])
        p1 = sb("p1", [P, 2, NODES])
        p1_t = sb("p1_t", [P, 2, TILES, P])
        pe_t = sb("pe_t", [P, TILES, P])
        pl_t = sb("pl_t", [P, TILES, P])
        o1 = sb("o1", [P, 2, H1, HID])
        parts = [sb(f"parts{c}", [SPLIT, NODES], BF16) for c in "el"]
        part_r = [sb(f"part_r{c}", [SPLIT, NODES]) for c in "el"]
        part_m = [sb(f"part_m{c}", [SPLIT, NODES], BF16) for c in "el"]
        ci = sb("ci", [P, TILES, H2])
        hw = sb("hw", [P, TILES, DIM])
        ul = sb("ul", [P, USLOTS, NODES])
        acc2 = sb("acc2", [P, 2, NODES])
        elu_y = sb("elu_y", [P, TILES, DIM])

        w_in = sem("w_in")
        adj_in = sem("adj_in"); x_loaded = sem("x_loaded"); stored = sem("stored")
        const_made = sem("const_made"); const_step = sem("const_step")
        prep_pe = sem("prep_pe"); prep_dve = sem("prep_dve"); table_in = sem("table_in")
        dve_passed = sem("dve_passed")
        step_e = sem("step_e"); step_l = sem("step_l"); step_m = sem("step_m")
        split_ready = [sem("split_e"), sem("split_l")]
        pool_passed = sem("pool_passed")
        mask1_ready = sem("mask1_ready"); maskn_ready = sem("maskn_ready"); maskl_ready = sem("maskl_ready"); masks0_ready = sem("masks0_ready")
        stats_ready = [sem("stats_e"), sem("stats_l")]
        rstd_ready = [sem("rstd_e"), sem("rstd_l")]
        xn_ready = [sem("xn_e"), sem("xn_l")]
        early_ready = sem("early_ready"); early_free = sem("early_free")
        turn_ready = sem("turn_ready"); turn_free = sem("turn_free")
        value_ready = sem("value_ready"); value_free = sem("value_free")
        hak_ready = sem("hak_ready")
        relu0_ready = sem("relu0_ready"); max0_ready = sem("max0_ready"); exp0_ready = sem("exp0_ready")
        recip0_ready = sem("recip0_ready"); xb_ready = sem("xb_ready")
        relu_act = sem("relu_act"); relu_dve = sem("relu_dve"); rounds_done = sem("rounds_done")
        raw_copied = sem("raw_copied"); mirrored = sem("mirrored"); ord_ready = sem("ord_ready"); ord_free = sem("ord_free")
        m1_ready = sem("m1_ready"); z1_ready = sem("z1_ready"); p1_ready = sem("p1_ready")
        p1t_ready = sem("p1t_ready"); p1t_act = sem("p1t_act"); p1t_dve = sem("p1t_dve")
        o1_ready = sem("o1_ready"); o1_recip = sem("o1_recip"); o1_scaled = sem("o1_scaled")
        x2_ready = sem("x2_ready"); xc_ready = sem("xc_ready")
        z_ready = sem("z_ready"); relul_ready = sem("relul_ready"); maxl_ready = sem("maxl_ready")
        expl_ready = sem("expl_ready"); recipl_ready = sem("recipl_ready"); recip3_ready = sem("recip3_ready"); acc_ready = sem("acc_ready")
        elu_in = sem("elu_in"); elu_exp = sem("elu_exp"); x4_ready = sem("x4_ready")

        block = ctx.enter_context(nc.Block())

        spread_f = e1[:, 0, :]

        @block.sync
        def _(sp):
            def load(k):
                since(sp, masks0_ready, k * KINDS)
                since(sp, maskn_ready, k)
                sp.dma_start(adj_i[:, :, :], adj[bass.ds(k, 1), :, :].rearrange(
                    "o (t p) j -> p (o t) j", p=P)).then_inc(adj_in, 16)
                since(sp, early_free, EARLY_USES.upto(k - 1, "attn3"))
                sp.dma_start(x_in[:, :, :], x[bass.ds(k, 1), :, :].rearrange(
                    "o (t p) d -> p (o t) d", p=P)).then_inc(x_loaded, 16)

            def store(k):
                sp.wait_ge(x4_ready, k + 1)
                sp.dma_start(out[bass.ds(k, 1), :, :].rearrange("o (t p) d -> p (o t) d", p=P),
                             x_out[:, :, :]).then_inc(stored, 16)

            load(0)
            for k in range(KINDS):
                sp.dma_start(ak_row[:, k:k + 1], a_k[k].rearrange("(d o) -> d o", o=1)).then_inc(w_in, 16)
            sp.dma_start(w1_sb[:, :], w1).then_inc(w_in, 16)
            sp.dma_start(w2_sb[:, :], w2).then_inc(w_in, 16)
            sp.dma_start(w3_sb[:, :], w3).then_inc(w_in, 16)
            sp.dma_start(aw_sb[:, :], a_w).then_inc(w_in, 16)
            sp.dma_start(b2_row[:, :], a_b.rearrange("(o h) -> o h", o=1).broadcast_to([P, H2])).then_inc(w_in, 16)
            sp.dma_start(a12[:, 0:1], a1.rearrange("(d o) -> d o", o=1)).then_inc(w_in, 16)
            sp.dma_start(a12[:, 1:2], a2.rearrange("(d o) -> d o", o=1)).then_inc(w_in, 16)
            sp.wait_ge(const_made, 1)
            for h in range(H1):
                sp.dma_start(wa_block[HID * h:HID * (h + 1), h:h + 1],
                             wa[h:h + 1, :].rearrange("o d -> d o")).then_inc(w_in, 16)
            load(1)
            load(2)
            with sp.Fori(3, BATCH) as k:
                load(k)
                store(k - 3)
            store(BATCH - 3)
            store(BATCH - 2)
            store(BATCH - 1)
            sp.wait_ge(stored, 16 * (BATCH + 1))

        W_LOADS = 16 * (KINDS + 7 + H1)
        CONST_MADE = 8

        @block.gpsimd
        def _(pool):
            g = nc.gpsimd
            g.memset(wa_block[:, :], 0.0).then_inc(const_made, 1)
            for t in (ident[:, :], ident_b[:, :], far_b[:, :], spread[:, :, :, :], reorder[:, :],
                      pick[:, :, :], pick1[:, :, :], head_block[:, :, :]):
                g.memset(t, 0.0).then_inc(const_step, 1)
            g.memset(half[:, :], -0.5).then_inc(const_made, 1)
            pool.wait_ge(const_step, 8)

            def one_where_zero(t, base, pattern, fill=1.0):
                return g.affine_select(out=t, in_=t, compare_op=ALU.not_equal, fill=fill, base=base,
                                       pattern=pattern, channel_multiplier=1)
            one_where_zero(ident[:, :], 0, [[-1, P]]).then_inc(const_made, 1)
            one_where_zero(ident_b[:, :], 0, [[-1, P]]).then_inc(const_made, 1)
            one_where_zero(far_b[:, :], 0, [[-1, P]], -NEG / SLOPE0).then_inc(const_made, 1)
            one_where_zero(spread[:, :, :, :], 0, [[-GROUP, PER_TILE], [0, H1], [-1, GROUP]]).then_inc(const_made, 1)
            one_where_zero(reorder[:, :].rearrange("p (h c s) -> p h c s", h=H1, c=4), 0,
                           [[-ROUNDS, H1], [-GROUP, 4], [-1, ROUNDS]]).then_inc(const_made, 1)
            for part in range(3):
                if part:
                    pool.wait_ge(const_step, 8 + 2 * part)
                one_where_zero(pick[:, :, :], -32 * part, [[-1, H2], [0, P]]).then_inc(const_step, 1)
                one_where_zero(pick1[:, :, :], -32 * part, [[-1, H1], [0, GROUP]]).then_inc(const_step, 1)
            pool.wait_ge(const_step, 14)
            g.memset(x_out[:, 0, 0:1], 1.0).then_inc(const_made, 1)

            def layernorm_apply(which, k, n, src):
                pool.wait_ge(stats_ready[which], 2 * k + n + 1)
                g.tensor_tensor(rstd[which][:, :], var_eps[which][:, :], half[:, :],
                                ALU.pow).then_inc(rstd_ready[which], 1)
                pool.wait_ge(rstd_ready[which], 2 * k + n + 1)
                pool.sem_inc(pool_passed, 1)
                for t in range(TILES):
                    ins = g.tensor_scalar(x_norm[which][:, t, :], src[:, t, :], mean_var[which][:, t, 0:1],
                                          rstd[which][:, t:t + 1], ALU.subtract, ALU.mult)
                ins.then_inc(xn_ready[which], 1)

            def split_low(which, count):
                def own(n, ins):
                    ins.then_inc(split_ready[which], 1)
                    pool.wait_ge(split_ready[which], count + n)
                    pool.sem_inc(pool_passed, 1)
                own(1, g.tensor_copy(part_m[which][:, :], part_r[which][:, :]))
                own(2, g.tensor_tensor(part_r[which][:, :], part_r[which][:, :], part_m[which][:, :], ALU.subtract))
                g.tensor_copy(parts[which][32:64, :], part_m[which][32:64, :]).then_inc(split_ready[which], 1)
                own(4, g.tensor_copy(parts[which][64:96, :], part_r[which][64:96, :]))

            def front(k):
                yield LN0 + 1
                since(pool, early_ready, EARLY_USES.upto(k - 1, "turn1"))
                layernorm_apply(0, k, 0, x_in)

            def early(k):
                yield 20
                since(pool, mask1_ready, k)
                pool.sem_inc(pool_passed, 1)
                g.tensor_scalar(mask_n[:, :, :], adj_i[:, :, :], 0, NEG, ALU.is_le, ALU.mult).then_inc(maskn_ready, 1)
                yield LN1
                layernorm_apply(0, k, 1, x_a)

            def masks(k):
                yield LN0 + 2
                since(pool, early_free, EARLY_USES.upto(k - 1, f"score{KINDS - 1}.{TILES - 1}"))
                pool.wait_ge(adj_in, 16 * k + 16)
                pool.sem_inc(pool_passed, 1)
                g.tensor_scalar(mask_one[:, :, :], adj_i[:, :, :], 1, 1.0, ALU.is_equal,
                                ALU.subtract).then_inc(masks0_ready, 1)
                for n in range(1, KINDS):
                    g.tensor_scalar(is_kind[:, n - 1, :, :], adj_i[:, :, :], n + 1, None,
                                    ALU.is_equal).then_inc(masks0_ready, 1)

            def late(k):
                for n, layer, src in ((0, 2, x_c), (1, 3, x_d)):
                    yield LN[layer] + 1
                    layernorm_apply(1, k, n, src)
                    yield LN[layer] + SPLITTED[layer] + 1
                    pool.wait_ge(value_free, VALUE_USES.upto(k, f"vec{layer}"))
                    pool.sem_inc(pool_passed, 1)
                    split_low(1, k * 8 + 4 * n)

            def layer1(b, has_late):
                yield LN[2] + SPLITTED[2] + 1
                since(pool, xc_ready, b)
                pool.wait_ge(early_free, EARLY_USES.upto(b, "attn3"))
                pool.sem_inc(pool_passed, 1)
                g.tensor_copy(x_b[:, :, :], x_a[:, :, :]).then_inc(xb_ready, 1)
                yield 19
                since(pool, m1_ready, b * GROUPS)
                if has_late:
                    pool.wait_ge(maskl_ready, b)
                pool.wait_ge(maskn_ready, b + 1)
                pool.sem_inc(pool_passed, 1)
                g.tensor_copy(mask_1[:, :, :], mask_n[:, :, :]).then_inc(mask1_ready, 1)
                yield 29
                pool.wait_ge(ord_free, ORD_USES.upto(b, "vec"))
                pool.sem_inc(pool_passed, 1)
                split_low(0, b * 4)

            def batch(b, has_late=True, has_early=True, has_front=True):
                chains = [Chain(late(b - 1))] * has_late + [Chain(layer1(b, has_late))] \
                    + [Chain(early(b + 1))] * has_early + [Chain(front(b + 2)), Chain(masks(b + 2))] * has_front
                for slot in range(LAST):
                    for chain in chains:
                        chain.run(slot)

            def alone(*parts):
                for part in parts:
                    Chain(part).run(LAST)

            alone(front(0), masks(0), early(0), front(1), masks(1))
            batch(0, has_late=False)
            with pool.Fori(1, BATCH - 2) as b:
                batch(b)
            batch(BATCH - 2, has_front=False)
            batch(BATCH - 1, has_early=False, has_front=False)
            alone(late(BATCH - 1))

        @block.scalar
        def _(act):
            s = nc.scalar
            act.wait_ge(const_made, CONST_MADE)
            s.activation(x_out[:, 0, 0:1], x_out[:, 0, 0:1], ACT.Exp).then_inc(table_in, 1)

            def front(k):
                yield SUMS + 6
                act.wait_ge(early_ready, EARLY_USES.upto(k, "turn0"))
                s.activation(h_t0[:, :], bank[7][:, :], ACT.Relu).then_inc(early_free, 1)

            def early(k, at=(7,) * KINDS):
                def use(name):
                    act.wait_ge(early_ready, EARLY_USES.upto(k, name))
                for t in range(TILES):
                    yield TILE0[t] + 1
                    use(f"score0.{t}")
                    s.copy(score0[:, t % 2, :], bank[at[0]][:, :]).then_inc(early_free, 1)
                    yield TILE0[t] + 11
                    act.wait_ge(early_free, EARLY_USES.upto(k, f"score{KINDS - 1}.{t}"))
                    s.activation(relu0[:, t % 2, :], score0[:, t % 2, :], ACT.Relu,
                                 scale=lift(SLOPE0)).then_inc(relu0_ready, 1)
                    yield TILE0[t] + 14
                    act.wait_ge(max0_ready, k * 4 + t + 1)
                    s.activation(score0[:, t % 2, :], score0[:, t % 2, :], ACT.Exp, scale=-1.0,
                                 bias=nmax0[:, t:t + 1], accum_out=rsum0[:, t:t + 1]).then_inc(exp0_ready, 1)
                    yield TILE0[t] + 16
                    use(f"pt{t}")
                    s.copy(pe_t[:, :, :].rearrange("p t i -> p (t i)"), bank[7][:, :]).then_inc(early_free, 1)
                yield LN1 + 8
                use("turn1")
                s.activation(h_t1[:, 0:NODES], bank[7][:, :], ACT.Relu)
                s.activation(h_t1[:, NODES:NODES + P], bank[7][:, 0:P], ACT.Relu).then_inc(early_free, 1)
                yield SUMS + 2
                use("yt")
                s.copy(y_t[:, 0:NODES], bank[7][:, :])
                s.copy(y_t[:, NODES:NODES + WIN], bank[7][:, 0:WIN]).then_inc(early_free, 1)

            def late(k):
                def turned(layer):
                    act.wait_ge(turn_ready, TURN_USES.upto(k, f"turn{layer}"))
                    s.activation(h_tl[:, :], bank[5][:, :], ACT.Relu).then_inc(turn_free, 1)

                def projected(layer):
                    act.wait_ge(value_ready, VALUE_USES.upto(k, f"proj{layer}"))
                    s.copy(hw[:, :, :].rearrange("p t d -> p (t d)"), bank[6][:, :]).then_inc(value_free, 1)

                def copy_pt(layer, t):
                    act.wait_ge(turn_ready, TURN_USES.upto(k, f"pt{layer}.{t}"))
                    s.copy(pl_t[:, :, :].rearrange("p t i -> p (t i)"), bank[5][:, :]).then_inc(turn_free, 1)

                def items(layer):
                    first = 0 if layer == 2 else ITEMS - TILES
                    last = ITEMS - TILES - 1 if layer == 2 else ITEMS - 1
                    for slot in range(ITEM[first] + RELU[layer], ITEM[last] + COPY[layer] + 1):
                        yield slot
                        for n in range(first, last + 1):
                            t, h = (n // H2, n % H2) if layer == 2 else (n - first, 0)
                            slope = SLOPE2 if layer == 2 else SLOPE3
                            if ITEM[n] + RELU[layer] == slot:
                                act.wait_ge(z_ready, k * ITEMS + n + 1)
                                if n == first:
                                    act.wait_ge(turn_free, TURN_USES.upto(k, f"ci{layer}"))
                                if n >= USLOTS:
                                    act.wait_ge(acc_ready, k * (ITEMS - TILES) + n - USLOTS + 1)
                                s.activation(ul[:, n % USLOTS, :], bank[zbank(n)][:, :], ACT.Relu,
                                             bias=ci[:, t, h:h + 1], scale=lift(slope)).then_inc(relul_ready, 1)
                            if ITEM[n] + EXP[layer] == slot:
                                act.wait_ge(maxl_ready, k * ITEMS + n + 1)
                                s.activation(ul[:, n % USLOTS, :], ul[:, n % USLOTS, :], ACT.Exp, scale=-1.0,
                                             bias=nmaxl[:, n:n + 1],
                                             accum_out=rsuml[:, n:n + 1]).then_inc(expl_ready, 1)
                            if (layer == 3 or h == H2 - 1) and ITEM[n] + COPY[layer] == slot:
                                copy_pt(layer, t)

                for layer in (2, 3):
                    yield LN[layer] + RELUED[layer]
                    turned(layer)
                    yield LN[layer] + SOURCED[layer] + 3
                    projected(layer)
                    yield from items(layer)
                yield END[3] + 2
                act.wait_ge(elu_in, k + 1)
                s.activation(x_out[:, :, :], x_out[:, :, :], ACT.Exp).then_inc(elu_exp, 1)

            def relus(b, slot):
                q, rnd = slot // ROUNDS, slot % ROUNDS
                if True in ON_ACT[4 * rnd:4 * rnd + 4]:
                    since(act, rounds_done, (b * GROUPS + q - 1) * ROUNDS + rnd + 1)
                for c in range(4):
                    if ON_ACT[4 * rnd + c]:
                        i = c * ROUNDS + rnd
                        s.activation(relu_s[:, i, 0:WINS[q]], y_t[:, q * GROUP:q * GROUP + WINS[q]], ACT.Relu,
                                     bias=y_t[:, q * GROUP + i:q * GROUP + i + 1]).then_inc(relu_act, 1)

            def early_relus(b, j):
                if j == RELU_ROW:
                    act.wait_ge(early_free, EARLY_USES.upto(b, "yt"))
                if RELU_ROW <= j < RELU_ROW + LEAD:
                    relus(b, j - RELU_ROW)

            def batch(b, has_late=True, has_early=True, has_front=True):
                chains = [Chain(late(b - 1))] * has_late + [Chain(early(b + 1))] * has_early \
                    + [Chain(front(b + 2))] * has_front

                def background(slot):
                    for chain in chains:
                        chain.run(slot)

                def copy_raw(q):
                    act.wait_ge(rounds_done, (b * GROUPS + q + 1) * ROUNDS)
                    if q >= 2:
                        act.wait_ge(ord_ready, ORD_USES.upto(b, f"ord{q - 2}"))
                    s.copy(d_raw[:, q % 2, 0:WINS[q]], bank[q % 2][:, 0:WINS[q]]).then_inc(raw_copied, 1)

                def copy_ord(q):
                    act.wait_ge(ord_ready, ORD_USES.upto(b, f"ord{q}"))
                    s.copy(e1[:, q, 0:WINS[q]], bank[2][:, 0:WINS[q]]).then_inc(ord_free, 1)

                for slot in range(SUMS):
                    q, rnd = slot // ROUNDS, slot % ROUNDS
                    if slot + LEAD < SUMS:
                        relus(b, slot + LEAD)
                    if rnd == 4 and q:
                        copy_raw(q - 1)
                    if rnd == 7 and q:
                        copy_ord(q - 1)
                    name = EXTRA.get(q, "")
                    if rnd == 3 and name.startswith("yrot"):
                        act.wait_ge(ord_ready, ORD_USES.upto(b, name))
                        s.copy(y_rot[:, int(name[4:]), :, :].rearrange("p t d -> p (t d)"),
                               bank[2][:, :]).then_inc(ord_free, 1)
                    background(slot)
                copy_raw(GROUPS - 1)
                for j in range(GROUPS):
                    if j == 1:
                        copy_ord(GROUPS - 1)
                    if j < GROUPS:
                        act.wait_ge(z1_ready, b * GROUPS + j + 1)
                        since(act, p1t_ready, b * GROUPS + j - 1)
                        q = ROW_ORDER[j]
                        s.activation(p1[:, j % 2, :], e1[:, q, :], ACT.Exp, scale=-1.0,
                                     bias=nmax1[:, q:q + 1], accum_out=rsum1[:, q:q + 1]).then_inc(p1_ready, 1)
                    if j >= 1 and (j - 1) % 2 == 0:
                        act.wait_ge(p1t_ready, b * GROUPS + j)
                        since(act, o1_ready, b * GROUPS + j - 2)
                        s.copy(p1_t[:, 0, :, :].rearrange("p t i -> p (t i)"), bank[1][:, :]).then_inc(p1t_act, 1)
                    background(SUMS + j)
                    if has_early:
                        early_relus(b + 1, j)
                background(LAST)

            def alone(part):
                Chain(part).run(LAST)

            alone(front(0))
            alone(early(0, FIRST_BANKS))
            alone(front(1))
            for j in range(GROUPS):
                early_relus(0, j)
            batch(0, has_late=False)
            with act.Fori(1, BATCH - 2) as b:
                batch(b)
            batch(BATCH - 2, has_front=False)
            batch(BATCH - 1, has_early=False, has_front=False)
            alone(late(BATCH - 1))

        @block.vector
        def _(dve):
            v_ = nc.vector
            dve.sem_inc(stored, 16)
            dve.wait_ge(const_made, CONST_MADE)
            dve.wait_ge(w_in, W_LOADS)
            v_.memset(slot_w[:, :, :, :], 0.0).then_inc(prep_dve, 1)
            v_.memset(v1[:, :], 0.0).then_inc(prep_dve, 1)
            v_.memset(v2j[:, :], 0.0).then_inc(prep_dve, 1)
            v_.memset(v3j[:, :], 0.0).then_inc(prep_dve, 1)
            v_.tensor_copy(spread_f, spread[:, :, :, :].rearrange("p v h i -> p (v h i)")).then_inc(prep_dve, 1)
            dve.wait_ge(prep_dve, 5)
            for h in range(H1):
                v_.memset(head_block[HID * h:HID * (h + 1), h, :], 1.0).then_inc(prep_dve, 1)
            for k in range(ROUNDS):
                v_.tensor_scalar(slot_w[:, k, :, k], wa_block[:, :], 1.0 - SLOPE1, None, ALU.mult).then_inc(prep_dve, 1)
            dve.wait_ge(prep_pe, 1)
            v_.tensor_copy(w1t[:, :], bank[0][:, 0:P]).then_inc(prep_dve, 1)
            v_.tensor_copy(w2t[:, :], bank[0][:, P:2 * P]).then_inc(prep_dve, 1)
            v_.tensor_copy(w3t[:, :], bank[0][:, 2 * P:3 * P]).then_inc(prep_dve, 1)
            v_.tensor_copy(awt[:, :, :].rearrange("p a h -> p (a h)"), bank[1][:, 0:2 * H2]).then_inc(prep_dve, 1)
            v_.tensor_copy(gather[:, :, :].rearrange("p v i -> p (v i)"), bank[2][:, :]).then_inc(prep_dve, 1)
            dve.wait_ge(prep_pe, 2)
            for part in range(3):
                c = 32 * part
                v_.tensor_scalar(v1[:, c:c + H1], bank[3][:, 0:H1], SLOPE1, None, ALU.mult).then_inc(prep_dve, 1)
                v_.tensor_copy(v2j[:, c:c + H2], bank[3][:, 16:16 + H2]).then_inc(prep_dve, 1)
                v_.tensor_copy(v3j[:, c:c + 1], bank[3][:, 33:34]).then_inc(prep_dve, 1)
            v_.tensor_scalar(v2i[:, :], bank[3][:, 8:8 + H2], lift(SLOPE2), None, ALU.mult).then_inc(prep_dve, 1)
            v_.tensor_scalar(v3i[:, :], bank[3][:, 32:33], lift(SLOPE3), None, ALU.mult).then_inc(prep_dve, 1)
            v_.tensor_scalar(b2_row[:, :], b2_row[:, :], lift(SLOPE2), None, ALU.mult).then_inc(prep_dve, 1)
            dve.wait_ge(prep_dve, 9 + ROUNDS + 5 + 12)

            def leaky(to, lifted, u, slope, nmax):
                dve.sem_inc(dve_passed, 1)
                return v_.tensor_tensor_reduce(to, lifted, u, -slope, BIG, ALU.add, ALU.min, nmax)

            def own(semaphore, count, ins):
                ins.then_inc(semaphore, 1)
                dve.wait_ge(semaphore, count)

            STEPS_E, STEPS_L, STEPS_M = 4, 7, 1

            def layernorm_stats(which, src, semaphore, count):
                for t in range(TILES):
                    ins = v_.bn_stats(stats[which][:, t, :], src[:, t, :])
                own(semaphore, count, ins)
                dve.sem_inc(dve_passed, 1)
                for t in range(TILES):
                    ins = v_.bn_aggr(mean_var[which][:, t, :], stats[which][:, t, :])
                own(semaphore, count + 1, ins)
                v_.tensor_scalar(var_eps[which][:, :], mean_var[which][:, :, 1], EPS, None,
                                 ALU.add).then_inc(stats_ready[which], 1)

            def split_high(which, src, semaphore, count):
                own(semaphore, count, v_.tensor_copy(parts[which][:, :], src))
                return v_.tensor_tensor(part_r[which][:, :], src, parts[which][:, :], ALU.subtract)

            def row_step(b, j):
                if 2 <= j < GROUPS + 2 and j % 2 == 1:
                    n = j - 2
                    dve.wait_ge(p1t_ready, b * GROUPS + n + 1)
                    since(dve, o1_ready, b * GROUPS + n - 1)
                    v_.tensor_copy(p1_t[:, 1, :, :].rearrange("p t i -> p (t i)"),
                                   bank[1][:, :]).then_inc(p1t_dve, 1)
                if j < GROUPS:
                    q = ROW_ORDER[j]
                    dve.wait_ge(mirrored, b * GROUPS + (q if q >= GROUPS // 2 else GROUPS))
                    dve.wait_ge(m1_ready, b * GROUPS + j + 1)
                    dve.sem_inc(dve_passed, 1)
                    v_.tensor_tensor_reduce(e1[:, q, :], e1[:, q, :], bank[0][:, :], -1.0, BIG, ALU.add,
                                            ALU.min, nmax1[:, q:q + 1]).then_inc(z1_ready, 1)
                if j >= 3:
                    n = j - 3
                    q = ROW_ORDER[n]
                    dve.wait_ge(p1_ready, b * GROUPS + n + 1)
                    v_.reciprocal(rinv1[:, q:q + 1], rsum1[:, q:q + 1]).then_inc(o1_recip, 1)
                    dve.wait_ge(o1_recip, b * GROUPS + n + 1)
                    dve.wait_ge(o1_ready, b * GROUPS + n + 1)
                    since(dve, x2_ready, b * GROUPS + n - 1)
                    v_.scalar_tensor_tensor(o1[:, n % 2, :, :], bank[3][:, None, 0:HID].broadcast_to([P, H1, HID]),
                                            rinv1[:, q:q + 1], head_block[:, :, :],
                                            ALU.mult, ALU.mult).then_inc(o1_scaled, 1)

            def front(k):
                yield LN0
                dve.wait_ge(x_loaded, 16 * k + 16)
                since(dve, xn_ready[0], 2 * k)
                layernorm_stats(0, x_in, step_e, k * STEPS_E + 1)
                yield SUMS + 4
                dve.wait_ge(xn_ready[0], 2 * k + 1)
                v_.tensor_scalar(h_row[:, :, :], x_norm[0][:, :, :], 0.0, None, ALU.max).then_inc(hak_ready, 1)
                yield SUMS + 7
                dve.wait_ge(early_free, EARLY_USES.upto(k, "turn0"))
                for n in range(KINDS):
                    v_.tensor_scalar(h_ak[:, n, :], h_t0[:, :], ak_row[:, n:n + 1], None,
                                     ALU.mult).then_inc(hak_ready, 1)

            def early(k, at=(7,) * KINDS):
                for t in range(TILES):
                    for n in range(1, KINDS):
                        yield TILE0[t] + 3 * n + 1
                        if t == 0:
                            dve.wait_ge(masks0_ready, k * KINDS + n + 1)
                        dve.wait_ge(early_free, EARLY_USES.upto(k, f"score{n - 1}.{t}"))
                        dve.wait_ge(early_ready, EARLY_USES.upto(k, f"score{n}.{t}"))
                        dve.sem_inc(dve_passed, 1)
                        v_.copy_predicated(score0[:, t % 2, :], is_kind[:, n - 1, t, :],
                                           bank[at[n]][:, :]).then_inc(early_free, 1)
                    yield TILE0[t] + 13
                    dve.wait_ge(relu0_ready, k * 4 + t + 1)
                    leaky(score0[:, t % 2, :], relu0[:, t % 2, :], score0[:, t % 2, :], SLOPE0,
                          nmax0[:, t:t + 1]).then_inc(max0_ready, 1)
                    yield TILE0[t] + 18
                    dve.wait_ge(exp0_ready, k * 4 + t + 1)
                    v_.reciprocal(rinv0[:, t:t + 1], rsum0[:, t:t + 1]).then_inc(recip0_ready, 1)
                    yield TILE0[t] + 19
                    dve.wait_ge(recip0_ready, k * 4 + t + 1)
                    dve.wait_ge(early_ready, EARLY_USES.upto(k, f"attn{t}"))
                    if t == 0:
                        since(dve, xb_ready, k)
                    v_.scalar_tensor_tensor(x_a[:, t, :], bank[7][:, 0:P], rinv0[:, t:t + 1], x_in[:, t, :],
                                            ALU.mult, ALU.add).then_inc(early_free, 1)
                yield LN1
                dve.wait_ge(early_free, EARLY_USES.upto(k, "attn3"))
                layernorm_stats(0, x_a, step_e, k * STEPS_E + 3)

            def late(k):
                def vectors(layer):
                    base = k * STEPS_L + (2 if layer == 2 else 5)
                    yield LN[layer] + SPLITTED[layer]
                    dve.wait_ge(value_ready, VALUE_USES.upto(k, f"vec{layer}"))
                    ins = split_high(1, bank[6][0:SPLIT, :], step_l, base + 1)
                    ins.then_inc(value_free, 1)
                    dve.wait_ge(turn_ready, TURN_USES.upto(k, f"ci{layer}"))
                    if layer == 2:
                        v_.tensor_tensor(ci[:, :, :], bank[5][:, 0:TILES * H2].rearrange("p (t h) -> p t h", h=H2),
                                         b2_row[:, None, :].broadcast_to([P, TILES, H2]),
                                         ALU.add).then_inc(turn_free, 1)
                    else:
                        v_.tensor_copy(ci[:, :, 0], bank[5][:, 0:TILES]).then_inc(turn_free, 1)

                yield 0
                v_.tensor_copy(mask_l[:, :, :], mask_1[:, :, :]).then_inc(maskl_ready, 1)
                for j in range(GROUPS, GROUPS + 3):
                    yield j - GROUPS
                    row_step(k, j)
                yield LN[2]
                dve.wait_ge(x2_ready, k * GROUPS + GROUPS)
                dve.wait_ge(xb_ready, k + 1)
                v_.tensor_tensor(x_c[:, :, :].rearrange("p t d -> p (t d)"), bank[2][:, :],
                                 x_b[:, :, :].rearrange("p t d -> p (t d)"), ALU.add).then_inc(xc_ready, 1)
                dve.wait_ge(xc_ready, k + 1)
                layernorm_stats(1, x_c, step_l, k * STEPS_L + 1)
                yield from vectors(2)
                for slot in range(ITEM2[0] + LEAKY[2], END[2] + 1):
                    yield slot
                    for n in range(ITEMS - TILES):
                        t, h = n // H2, n % H2
                        u = ul[:, n % USLOTS, :]
                        at = acc2[:, t % 2, :]
                        if ITEM[n] + LEAKY[2] == slot:
                            dve.wait_ge(relul_ready, k * ITEMS + n + 1)
                            leaky(u, u, bank[zbank(n)][:, :], SLOPE2, nmaxl[:, n:n + 1]).then_inc(maxl_ready, 1)
                        if ITEM[n] + SUM[2] - 1 == slot:
                            dve.wait_ge(expl_ready, k * ITEMS + n + 1)
                            v_.reciprocal(rinvl[:, n:n + 1], rsuml[:, n:n + 1]).then_inc(recipl_ready, 1)
                        if ITEM[n] + SUM[2] == slot:
                            dve.wait_ge(recipl_ready, k * 32 + n + 1)
                            if h == 0:
                                if t >= 2:
                                    dve.wait_ge(turn_ready, TURN_USES.upto(k, f"pt2.{t - 2}"))
                                v_.tensor_scalar(at, u, rinvl[:, n:n + 1], None, ALU.mult).then_inc(acc_ready, 1)
                            else:
                                dve.wait_ge(acc_ready, k * (ITEMS - TILES) + n)
                                v_.scalar_tensor_tensor(at, u, rinvl[:, n:n + 1], at, ALU.mult,
                                                        ALU.add).then_inc(acc_ready, 1)
                        if h == H2 - 1 and ITEM[n] + ADD[2] == slot:
                            dve.wait_ge(value_ready, VALUE_USES.upto(k, f"attn2.{t}"))
                            v_.scalar_tensor_tensor(x_d[:, t, :], bank[6][:, 0:P], 1.0 / H2, x_c[:, t, :],
                                                    ALU.mult, ALU.add).then_inc(value_free, 1)
                yield LN[3]
                dve.wait_ge(value_free, VALUE_USES.upto(k, "attn2.3"))
                layernorm_stats(1, x_d, step_l, k * STEPS_L + 4)
                yield from vectors(3)
                for slot in range(ITEM3[0] + LEAKY[3], END[3] + 1):
                    yield slot
                    for t in range(TILES):
                        n = ITEMS - TILES + t
                        u = ul[:, n % USLOTS, :]
                        if ITEM[n] + LEAKY[3] == slot:
                            dve.wait_ge(relul_ready, k * ITEMS + n + 1)
                            leaky(u, u, bank[zbank(n)][:, :], SLOPE3, nmaxl[:, n:n + 1]).then_inc(maxl_ready, 1)
                        if ITEM[n] + ADD[3] - 1 == slot:
                            dve.wait_ge(expl_ready, k * ITEMS + n + 1)
                            v_.reciprocal(rinvl[:, n:n + 1], rsuml[:, n:n + 1]).then_inc(recip3_ready, 1)
                        if ITEM[n] + ADD[3] == slot:
                            dve.wait_ge(recip3_ready, k * 4 + t + 1)
                            dve.wait_ge(value_ready, VALUE_USES.upto(k, f"attn3.{t}"))
                            v_.tensor_scalar(elu_y[:, t, :], bank[6][:, 0:P], rinvl[:, n:n + 1], None,
                                             ALU.mult).then_inc(value_free, 1)
                yield END[3] + 1
                dve.wait_ge(value_free, VALUE_USES.upto(k, "attn3.3"))
                dve.wait_ge(stored, 16 * k + 16)
                v_.tensor_scalar(x_out[:, :, :], elu_y[:, :, :], 0.0, None, ALU.min).then_inc(elu_in, 1)
                own(step_l, k * STEPS_L + 7, v_.scalar_tensor_tensor(
                    elu_y[:, :, :].rearrange("p t d -> p (t d)"), elu_y[:, :, :].rearrange("p t d -> p (t d)"), 0.0,
                    x_d[:, :, :].rearrange("p t d -> p (t d)"), ALU.max, ALU.add))
                yield END[3] + 2
                dve.wait_ge(elu_exp, k + 1)
                v_.scalar_tensor_tensor(x_out[:, :, :].rearrange("p t d -> p (t d)"),
                                        x_out[:, :, :].rearrange("p t d -> p (t d)"), -1.0,
                                        elu_y[:, :, :].rearrange("p t d -> p (t d)"), ALU.add,
                                        ALU.add).then_inc(x4_ready, 1)

            def relus(b, slot):
                q, rnd = slot // ROUNDS, slot % ROUNDS
                since(dve, rounds_done, (b * GROUPS + q - 1) * ROUNDS + rnd + 1)
                for c in range(4):
                    if not ON_ACT[4 * rnd + c]:
                        i = c * ROUNDS + rnd
                        v_.tensor_scalar(relu_s[:, i, 0:WINS[q]], y_t[:, q * GROUP:q * GROUP + WINS[q]],
                                         y_t[:, q * GROUP + i:q * GROUP + i + 1], 0.0, ALU.add,
                                         ALU.max).then_inc(relu_dve, 1)

            def early_relus(b, j):
                if j == RELU_ROW:
                    dve.wait_ge(early_free, EARLY_USES.upto(b, "yt"))
                if RELU_ROW <= j < RELU_ROW + LEAD:
                    relus(b, j - RELU_ROW)

            def batch(b, has_late=True, has_early=True, has_front=True):
                chains = [Chain(late(b - 1))] * has_late + [Chain(early(b + 1))] * has_early \
                    + [Chain(front(b + 2))] * has_front

                def background(slot):
                    for chain in chains:
                        chain.run(slot)

                def mirror(q):
                    dve.wait_ge(ord_free, ORD_USES.upto(b, f"ord{q}"))
                    flat = e1[:, :, :].rearrange("p q j -> p (q j)")
                    met = WINS[q] // GROUP - 1
                    inside = min(met, GROUPS - 1 - q)
                    for first, count, row in ((1, inside, q + 1), (inside + 1, met - inside, q + inside + 1 - GROUPS)):
                        if count:
                            at = row * NODES + NODES - GROUP * first
                            stride = NODES - GROUP
                            ins = v_.transpose(blocks(flat, at, count, stride),
                                               e1[:, q, GROUP * first:GROUP * (first + count)].rearrange(
                                                   "p (m c) -> p m c", c=GROUP))
                    ins.then_inc(mirrored, 1)

                def blocks(flat, at, count, stride):
                    if at + count * stride <= GROUPS * NODES:
                        return flat[:, at:at + count * stride].rearrange("p (m c) -> p m c", c=stride)[:, :, 0:GROUP]
                    at -= stride - GROUP
                    return flat[:, at:at + count * stride].rearrange("p (m c) -> p m c", c=stride)[
                        :, :, stride - GROUP:stride]

                for slot in range(SUMS):
                    q, rnd = slot // ROUNDS, slot % ROUNDS
                    if rnd == 3 and EXTRA.get(q) == "vec":
                        dve.wait_ge(ord_ready, ORD_USES.upto(b, "vec"))
                        split_high(0, bank[2][0:SPLIT, :], step_m, b * STEPS_M + 1).then_inc(ord_free, 1)
                    if slot + LEAD < SUMS:
                        relus(b, slot + LEAD)
                    if rnd == 1 and q >= 2:
                        mirror(q - 2)
                    background(slot)
                for j in range(GROUPS):
                    row_step(b, j)
                    if j == 0 or j == 2:
                        mirror(GROUPS - 2 + j // 2)
                    background(SUMS + j)
                    if has_early:
                        early_relus(b + 1, j)

            def alone(part):
                Chain(part).run(LAST)

            alone(front(0))
            alone(early(0, FIRST_BANKS))
            alone(front(1))
            for j in range(GROUPS):
                early_relus(0, j)
            batch(0, has_late=False)
            with dve.Fori(1, BATCH - 2) as b:
                batch(b)
            batch(BATCH - 2, has_front=False)
            batch(BATCH - 1, has_early=False, has_front=False)
            alone(late(BATCH - 1))

        @block.tensor
        def _(pe):
            T = nc.tensor

            def mm(o, l, r, start=True, stop=True):
                return T.matmul(o, l, r, start=start, stop=stop, skip_group_check=True)

            pe.wait_ge(const_made, CONST_MADE)
            pe.wait_ge(w_in, W_LOADS)
            pe.wait_ge(prep_dve, 5)
            for n, w in enumerate((w1_sb, w2_sb, w3_sb)):
                T.transpose(bank[0][:, n * P:(n + 1) * P], w[:, :], ident[:, :])
            for n in range(2):
                T.transpose(bank[1][:, n * H2:(n + 1) * H2], aw_sb[:, n * DIM:(n + 1) * DIM], ident[0:H2, 0:H2])
            for v in range(PER_TILE):
                ins = T.transpose(bank[2][:, v * P:(v + 1) * P], spread_f[:, v * P:(v + 1) * P], ident[:, :])
            ins.then_inc(prep_pe, 1)
            pe.wait_ge(prep_dve, 9 + ROUNDS + 5)
            mm(bank[3][:, 0:H1], w1t[:, :], wa_block[:, :])
            mm(bank[3][:, 8:8 + H2], w2t[:, :], awt[:, 0, :])
            mm(bank[3][:, 16:16 + H2], w2t[:, :], awt[:, 1, :])
            mm(bank[3][:, 32:34], w3_sb[:, :], a12[:, :]).then_inc(prep_pe, 1)
            pe.wait_ge(prep_dve, 9 + ROUNDS + 5 + 12)

            def turn(to, src):
                for t in range(TILES):
                    ins = T.transpose(to[:, t * P:(t + 1) * P], src[:, t * P:(t + 1) * P], ident[:, :])
                return ins

            def rows(t3):
                return t3.rearrange("p t d -> p (t d)")

            def attend(to, weights, values):
                for t in range(TILES):
                    ins = mm(to, weights[:, t, :], values[:, t, :], t == 0, t == TILES - 1)
                return ins

            def row_mask(b, j):
                q = ROW_ORDER[j]
                if j:
                    pe.wait_ge(z1_ready, b * GROUPS + j)
                else:
                    pe.wait_ge(raw_copied, b * GROUPS + GROUPS - 1)
                    pe.wait_ge(split_ready[0], 4 * b + 4)
                    pe.wait_ge(mask1_ready, b + 1)
                at = q * GROUP
                head = NODES - at
                lhs = spread[:, q % PER_TILE, :, :].rearrange("p h i -> p (h i)")
                picked = pick1[:, :, :].rearrange("p h i -> p (h i)")
                mask = mask_1[:, q // PER_TILE, :]
                mm(bank[0][:, 0:head], lhs, mask[:, at:NODES], True, False)
                if at:
                    mm(bank[0][:, head:NODES], lhs, mask[:, 0:at], False, False)
                ins = mm(bank[0][:, 0:head], picked, parts[0][:, at:NODES], False, True)
                if at:
                    ins = mm(bank[0][:, head:NODES], picked, parts[0][:, 0:at], False, True)
                ins.then_inc(m1_ready, 1)

            def row_step(b, j):
                if 1 <= j <= GROUPS:
                    n = j - 1
                    pe.wait_ge(p1_ready, b * GROUPS + n + 1)
                    if n >= 1:
                        pe.wait_ge((p1t_act, p1t_dve)[(n - 1) % 2], b * 8 + (n - 1) // 2 + 1)
                    turn(bank[1], p1[:, n % 2, :]).then_inc(p1t_ready, 1)
                if j < GROUPS - 1:
                    row_mask(b, j + 1)
                if 2 <= j <= GROUPS + 1:
                    n = j - 2
                    q = ROW_ORDER[n]
                    pe.wait_ge((p1t_act, p1t_dve)[n % 2], b * 8 + n // 2 + 1)
                    if n >= 1:
                        pe.wait_ge(o1_scaled, b * GROUPS + n)
                    for t in range(TILES):
                        for h in range(H1):
                            own = slice(GROUP * h, GROUP * (h + 1))
                            ins = mm(bank[3][own, 0:HID], p1_t[:, n % 2, t, own],
                                     y_rot[:, q % PER_TILE, (q // PER_TILE + t) % TILES, HID * h:HID * (h + 1)],
                                     t == 0, t == TILES - 1)
                    ins.then_inc(o1_ready, 1)
                if j >= 3:
                    n = j - 3
                    q = ROW_ORDER[n]
                    pe.wait_ge(o1_scaled, b * GROUPS + n + 1)
                    if n == 0:
                        pe.wait_ge(ord_free, ORD_USES.upto(b, f"ord{GROUPS - 1}"))
                    tile = q // PER_TILE
                    mm(bank[2][:, tile * P:(tile + 1) * P], gather[:, q % PER_TILE, :],
                       o1[:, n % 2, :, :].rearrange("p h d -> p (h d)"), q % PER_TILE == 0,
                       q % PER_TILE == PER_TILE - 1).then_inc(x2_ready, 1)

            def front(k):
                yield SUMS + 5
                pe.wait_ge(xn_ready[0], 2 * k + 1)
                since(pe, early_free, EARLY_USES.before(k, "turn0"))
                turn(bank[7], rows(x_norm[0][:, :, :])).then_inc(early_ready, 1)

            def early(k, at=(7,) * KINDS):
                def free(name):
                    since(pe, early_free, EARLY_USES.before(k, name))

                for t in range(TILES):
                    for n in range(KINDS):
                        yield TILE0[t] + 3 * n
                        pe.wait_ge(hak_ready, k * 5 + 1 + n + 1)
                        if n == 0:
                            pe.wait_ge(masks0_ready, k * KINDS + 1)
                        if n == 0 or at[n] == 7:
                            free(f"score{n}.{t}")
                        ins = mm(bank[at[n]][:, :], h_ak[:, n, t * P:(t + 1) * P], h_t0[:, :], True, n > 0)
                        if n == 0:
                            ins = mm(bank[at[n]][:, :], far_b[:, :], mask_one[:, t, :], False, True)
                        ins.then_inc(early_ready, 1)
                    yield TILE0[t] + 15
                    pe.wait_ge(exp0_ready, k * 4 + t + 1)
                    free(f"pt{t}")
                    turn(bank[7], score0[:, t % 2, :]).then_inc(early_ready, 1)
                    yield TILE0[t] + 17
                    free(f"attn{t}")
                    attend(bank[7][:, 0:P], pe_t, h_row).then_inc(early_ready, 1)
                yield LN1 + 6
                pe.wait_ge(xn_ready[0], 2 * k + 2)
                free("turn1")
                turn(bank[7], rows(x_norm[0][:, :, :])).then_inc(early_ready, 1)
                yield SUMS + 1
                free("yt")
                mm(bank[7][:, :], w1_sb[:, :], h_t1[:, 0:NODES]).then_inc(early_ready, 1)

            def late(k):
                def turn_free_of(name):
                    since(pe, turn_free, TURN_USES.before(k, name))

                def value_free_of(name):
                    since(pe, value_free, VALUE_USES.before(k, name))

                def front(layer, vj, vi, width, w):
                    n = layer - 2
                    yield LN[layer] + TURNED[layer]
                    pe.wait_ge(xn_ready[1], 2 * k + n + 1)
                    if layer == 3:
                        turn_free_of("turn3")
                    turn(bank[5], rows(x_norm[1][:, :, :])).then_inc(turn_ready, 1)
                    yield LN[layer] + SOURCED[layer]
                    pe.wait_ge(turn_free, TURN_USES.upto(k, f"turn{layer}"))
                    if layer == 3:
                        value_free_of("vec3")
                    mm(bank[6][0:SPLIT, :], vj, h_tl[:, :]).then_inc(value_ready, 1)
                    for t in range(TILES):
                        ins = mm(bank[5][:, t * width:(t + 1) * width], h_tl[:, t * P:(t + 1) * P], vi)
                    ins.then_inc(turn_ready, 1)
                    yield LN[layer] + SOURCED[layer]
                    value_free_of(f"proj{layer}")
                    for t in range(TILES):
                        ins = mm(bank[6][:, t * P:(t + 1) * P], h_tl[:, t * P:(t + 1) * P], w)
                    ins.then_inc(value_ready, 1)

                def scores(n, t, h):
                    if n >= len(ITEM2):
                        pe.wait_ge(maxl_ready, k * ITEMS + n)
                    elif n >= 2:
                        pe.wait_ge(maxl_ready, k * ITEMS + n - 1)
                    mm(bank[zbank(n)][:, :], pick[:, h, :], parts[1][:, :], True, False)
                    mm(bank[zbank(n)][:, :], ident_b[:, :], mask_l[:, t, :], False, True).then_inc(z_ready, 1)

                for j in range(GROUPS, GROUPS + 3):
                    yield j - GROUPS
                    row_step(k, j)
                yield from front(2, v2j[:, :], v2i[:, :], H2, w2_sb[:, :])
                for slot in range(ITEM2[0], END[2]):
                    yield slot
                    for n in range(ITEMS - TILES):
                        t, h = n // H2, n % H2
                        if ITEM[n] == slot:
                            if n == 0:
                                pe.wait_ge(split_ready[1], 8 * k + 4)
                                pe.wait_ge(maskl_ready, k + 1)
                            scores(n, t, h)
                        if h == H2 - 1 and ITEM[n] + TURN[2] == slot:
                            pe.wait_ge(acc_ready, k * (ITEMS - TILES) + n + 1)
                            turn_free_of(f"pt2.{t}")
                            turn(bank[5], acc2[:, t % 2, :]).then_inc(turn_ready, 1)
                        if h == H2 - 1 and ITEM[n] + ATTEND[2] == slot:
                            pe.wait_ge(turn_free, TURN_USES.upto(k, f"pt2.{t}"))
                            value_free_of(f"attn2.{t}")
                            attend(bank[6][:, 0:P], pl_t, hw).then_inc(value_ready, 1)
                yield from front(3, v3j[:, :], v3i[:, :], 1, w3t[:, :])
                for slot in range(ITEM3[0], END[3]):
                    yield slot
                    for t in range(TILES):
                        n = ITEMS - TILES + t
                        if ITEM[n] == slot:
                            if t == 0:
                                pe.wait_ge(split_ready[1], 8 * k + 8)
                            scores(n, t, 0)
                        if ITEM[n] + TURN[3] == slot:
                            pe.wait_ge(expl_ready, k * ITEMS + n + 1)
                            turn_free_of(f"pt3.{t}")
                            turn(bank[5], ul[:, n % USLOTS, :]).then_inc(turn_ready, 1)
                        if ITEM[n] + ATTEND[3] == slot:
                            pe.wait_ge(turn_free, TURN_USES.upto(k, f"pt3.{t}"))
                            value_free_of(f"attn3.{t}")
                            attend(bank[6][:, 0:P], pl_t, hw).then_inc(value_ready, 1)

            def batch(b, has_late=True, has_early=True, has_front=True):
                chains = [Chain(late(b - 1))] * has_late + [Chain(early(b + 1))] * has_early \
                    + [Chain(front(b + 2))] * has_front

                def background(slot):
                    for chain in chains:
                        chain.run(slot)

                def free(name):
                    since(pe, ord_free, ORD_USES.before(b, name))

                def put_in_order(q):
                    pe.wait_ge(raw_copied, b * GROUPS + q + 1)
                    free(f"ord{q}")
                    if q == 0:
                        since(pe, xc_ready, b)
                    mm(bank[2][:, 0:WINS[q]], reorder[:, :], d_raw[:, q % 2, 0:WINS[q]]).then_inc(ord_ready, 1)

                for slot in range(SUMS):
                    q, rnd = slot // ROUNDS, slot % ROUNDS
                    background(slot)
                    if rnd == 0:
                        if q >= 2:
                            pe.wait_ge(raw_copied, b * GROUPS + q - 1)
                        elif q == 0:
                            since(pe, z1_ready, b * GROUPS)
                    on_act = sum(ON_ACT[0:4 * rnd + 4])
                    since(pe, relu_act, (b * GROUPS + q) * ACT_SHARE + on_act)
                    since(pe, relu_dve, (b * GROUPS + q) * (GROUP - ACT_SHARE) + 4 * rnd + 4 - on_act)
                    for c in range(4):
                        ins = mm(bank[q % 2][32 * c:32 * c + 32, 0:WINS[q]],
                                 slot_w[:, rnd, :, :].rearrange("p h s -> p (h s)"),
                                 relu_s[:, c * ROUNDS + rnd, 0:WINS[q]], rnd == 0, rnd == ROUNDS - 1)
                    ins.then_inc(rounds_done, 1)
                    name = EXTRA.get(q, "")
                    if rnd == 1 and name:
                        free(name)
                        if name == "vec":
                            ins = mm(bank[2][0:SPLIT, :], v1[:, :], h_t1[:, 0:NODES])
                        else:
                            for t in range(TILES):
                                at = int(name[4:]) * GROUP + t * P
                                ins = mm(bank[2][:, t * P:(t + 1) * P], h_t1[:, at:at + P], w1_sb[:, :])
                        ins.then_inc(ord_ready, 1)
                    if rnd == 5 and q:
                        put_in_order(q - 1)
                    if slot == SUMS - 2:
                        row_mask(b, 0)
                put_in_order(GROUPS - 1)
                if has_late:
                    pe.wait_ge(maxl_ready, (b - 1) * ITEMS + len(ITEM2))
                for j in range(GROUPS):
                    row_step(b, j)
                    background(SUMS + j)

            def alone(part):
                Chain(part).run(LAST)

            alone(front(0))
            alone(early(0, FIRST_BANKS))
            alone(front(1))
            batch(0, has_late=False)
            with pe.Fori(1, BATCH - 2) as b:
                batch(b)
            batch(BATCH - 2, has_front=False)
            batch(BATCH - 1, has_early=False, has_front=False)
            alone(late(BATCH - 1))


INPUTS = ["x", "adj", "L0_gnn_a_0", "L0_gnn_a_1", "L0_gnn_a_2", "L0_gnn_a_3", "L1_gnn_W", "L1_gnn_Wa",
          "L2_gnn_W", "L2_gnn_a_w", "L2_gnn_a_b", "L3_gnn_W", "L3_gnn_a1", "L3_gnn_a2"]


def kernel(**inputs):
    import concourse.bacc as bacc
    from concourse.bass_utils import run_bass_kernel_spmd

    nc = bacc.Bacc("TRN2", target_bir_lowering=False, num_devices=1)
    arrays, d = {}, {}
    for name in INPUTS:
        a = np.ascontiguousarray(inputs[name])
        arrays[f"in_{name}"] = a
        d[name] = nc.dram_tensor(f"in_{name}", a.shape, mybir.dt.from_np(a.dtype), kind="ExternalInput").ap()
    out = nc.dram_tensor("out_0", (BATCH, NODES, DIM), F32, kind="ExternalOutput").ap()
    build(nc, d["x"], d["adj"], [d[f"L0_gnn_a_{k}"] for k in range(KINDS)], d["L1_gnn_W"], d["L1_gnn_Wa"],
          d["L2_gnn_W"], d["L2_gnn_a_w"], d["L2_gnn_a_b"], d["L3_gnn_W"], d["L3_gnn_a1"], d["L3_gnn_a2"], out)
    r = run_bass_kernel_spmd(nc, [arrays], core_ids=[0])
    return r.results[0]["out_0"]
```
